# Optimizing a Trainium2 kernel written in Bass

```python
import numpy as np
import jax
import jax.numpy as jnp

def _softmax(x, axis=-1):
    return jax.nn.softmax(x, axis=axis)

def _gelu(x):
    return jax.nn.gelu(x, approximate=True)

def _silu(x):
    return jax.nn.silu(x)

def _sigmoid(x):
    return jax.nn.sigmoid(x)

def _layernorm(x, axis=-1, eps=1e-05):
    m = jnp.mean(x, axis=axis, keepdims=True)
    v = jnp.var(x, axis=axis, keepdims=True)
    return (x - m) / jnp.sqrt(v + eps)

def _scatter_add(tgt, idx, src, axis=0):
    return tgt.at[idx].add(src)

def _segment_sum(src, seg, n):
    return jax.ops.segment_sum(src, seg, n)
kernel_name = 'mk_gnn_ffn_d1_gnn_r32_b158f8'

def setup_inputs(seed: int=0):
    np.random.seed(seed)
    _w = jnp.asarray

    def _rec_inputs():
        import jax
        import jax.numpy as jnp
        _gk = jax.random.key(seed)
        x = -0.0002117 + 1 * jax.random.normal(jax.random.fold_in(_gk, 1), (3125, 256), jnp.float32)
        src = jax.random.randint(jax.random.fold_in(_gk, 2), (50000,), 0, 3125, jnp.int32)
        dst = jax.random.randint(jax.random.fold_in(_gk, 3), (50000,), 0, 3125, jnp.int32)
        _o = jnp.argsort(dst, stable=True)
        src = src[_o]
        dst = dst[_o]
        edge_weight = jax.random.uniform(jax.random.fold_in(_gk, 12), (50000,), jnp.float32, 0.0, 1)
        return (x, src, dst, edge_weight)
    x, src, dst, edge_weight = _rec_inputs()

    def _L0_gnn_setup():
        import jax, jax.numpy as jnp
        import numpy as np
        N_NODES = 3125
        N_EDGES = 100000
        D_IN = 256
        D_OUT = 256
        key = jax.random.key(seed)
        k1, k2, k3, k4, k5, k6 = jax.random.split(key, 6)
        x = jax.random.normal(k1, (N_NODES, D_IN), dtype=jnp.float32)
        edge_src = jax.random.randint(k2, (N_EDGES,), 0, N_NODES, dtype=jnp.int64)
        edge_dst = jax.random.randint(k3, (N_EDGES,), 0, N_NODES, dtype=jnp.int64)
        adj_vals = jax.random.uniform(k4, (N_EDGES,), dtype=jnp.float32)
        bound = 2.0 * np.sqrt(6.0 / (D_IN + D_OUT))
        w_nbr = jax.random.uniform(k5, (D_IN, D_OUT), dtype=jnp.float32, minval=-bound, maxval=bound)
        w_own = jax.random.uniform(k6, (D_IN, D_OUT), dtype=jnp.float32, minval=-bound, maxval=bound)
        bias = jnp.zeros((D_OUT,), dtype=jnp.float32)
        return {'x': x, 'edge_src': edge_src, 'edge_dst': edge_dst, 'adj_vals': adj_vals, 'w_nbr': w_nbr, 'w_own': w_own, 'bias': bias}
    _L0_gnn_all = _L0_gnn_setup()
    _L0_gnn_in = {k: v for k, v in _L0_gnn_all.items() if k in ('w_nbr', 'w_own', 'bias')}
    del _L0_gnn_all

    def _L0_ffn_setup():
        import jax, jax.numpy as jnp
        import numpy as np
        TOP_K = 2
        LN_EPS = 1e-05
        key = jax.random.key(seed)
        ks = jax.random.split(key, 8)
        B, S, D, E, H = (16, 1024, 256, 8, 1024)
        x = jax.random.normal(ks[0], (B, S, D), dtype=jnp.float32)
        Wr = jax.random.normal(ks[1], (D, E), dtype=jnp.float32) * 0.1
        br = jnp.zeros((E,), dtype=jnp.float32)
        ln_g = jnp.ones((E, D), dtype=jnp.float32)
        ln_b = jnp.zeros((E, D), dtype=jnp.float32)
        W1 = jax.random.normal(ks[2], (E, D, H), dtype=jnp.float32) * (1.0 / np.sqrt(D))
        b1 = jnp.zeros((E, H), dtype=jnp.float32)
        W2 = jax.random.normal(ks[3], (E, H, D), dtype=jnp.float32) * (1.0 / np.sqrt(H))
        b2 = jnp.zeros((E, D), dtype=jnp.float32)
        return {'x': x, 'Wr': Wr, 'br': br, 'ln_g': ln_g, 'ln_b': ln_b, 'W1': W1, 'b1': b1, 'W2': W2, 'b2': b2}
    _L0_ffn_all = _L0_ffn_setup()
    _L0_ffn_in = {k: v for k, v in _L0_ffn_all.items() if k in ('Wr', 'br', 'ln_g', 'ln_b', 'W1', 'b1', 'W2', 'b2')}
    del _L0_ffn_all
    return {'x': x, 'src': src, 'dst': dst, 'edge_weight': edge_weight, 'L0_gnn_w_nbr': _L0_gnn_in['w_nbr'], 'L0_gnn_w_own': _L0_gnn_in['w_own'], 'L0_gnn_bias': _L0_gnn_in['bias'], 'L0_ffn_Wr': _L0_ffn_in['Wr'], 'L0_ffn_br': _L0_ffn_in['br'], 'L0_ffn_ln_g': _L0_ffn_in['ln_g'], 'L0_ffn_ln_b': _L0_ffn_in['ln_b'], 'L0_ffn_W1': _L0_ffn_in['W1'], 'L0_ffn_b1': _L0_ffn_in['b1'], 'L0_ffn_W2': _L0_ffn_in['W2'], 'L0_ffn_b2': _L0_ffn_in['b2']}

def reference(x, src, dst, edge_weight, L0_gnn_w_nbr, L0_gnn_w_own, L0_gnn_bias, L0_ffn_Wr, L0_ffn_br, L0_ffn_ln_g, L0_ffn_ln_b, L0_ffn_W1, L0_ffn_b1, L0_ffn_W2, L0_ffn_b2):
    import jax
    import jax.numpy as jnp

    def _L0_gnn_ref(x, edge_src, edge_dst, adj_vals, w_nbr, w_own, bias):
        import jax, jax.numpy as jnp
        import numpy as np
        N_NODES = 3125
        N_EDGES = 100000
        D_IN = 256
        D_OUT = 256
        h = x @ w_nbr
        msgs = adj_vals[:, None] * h[edge_src]
        agg = jax.ops.segment_sum(msgs, edge_dst, num_segments=x.shape[0])
        return agg + x @ w_own + bias

    def _L0_ffn_ref(x, Wr, br, ln_g, ln_b, W1, b1, W2, b2):
        import jax, jax.numpy as jnp
        import numpy as np
        TOP_K = 2
        LN_EPS = 1e-05
        B, S, D = x.shape
        N = B * S
        xt = x.reshape(N, D)
        logits = xt @ Wr + br
        probs = jax.nn.softmax(logits, axis=-1)
        top_p, top_idx = jax.lax.top_k(probs, TOP_K)
        weights = top_p / top_p.sum(axis=-1, keepdims=True)
        mu = xt.mean(axis=-1, keepdims=True)
        var = ((xt - mu) ** 2).mean(axis=-1, keepdims=True)
        xn = (xt - mu) * jax.lax.rsqrt(var + LN_EPS)
        xe = xn[None, :, :] * ln_g[:, None, :] + ln_b[:, None, :]
        h = jax.nn.gelu(jnp.einsum('end,edh->enh', xe, W1) + b1[:, None, :], approximate=False)
        y = jnp.einsum('enh,ehd->end', h, W2) + b2[:, None, :]
        y_tok = jnp.transpose(y, (1, 0, 2))
        sel = jnp.take_along_axis(y_tok, top_idx[:, :, None], axis=1)
        out = (weights[:, :, None] * sel).sum(axis=1)
        return out.reshape(B, S, D)
    x = x + _L0_gnn_ref(_layernorm(x, axis=-1), src, dst, edge_weight, L0_gnn_w_nbr, L0_gnn_w_own, L0_gnn_bias)
    x = x + _L0_ffn_ref(_layernorm(x, axis=-1)[None], L0_ffn_Wr, L0_ffn_br, L0_ffn_ln_g, L0_ffn_ln_b, L0_ffn_W1, L0_ffn_b1, L0_ffn_W2, L0_ffn_b2)[0]
    return x

_drawn_inputs = setup_inputs


def setup_inputs(seed=0):
    import zlib

    import numpy as np

    out = dict(_drawn_inputs(seed))
    spreads = {'L0_gnn_bias': (0.0, 0.362),
     'L0_ffn_br': (0.0, 0.334),
     'L0_ffn_ln_g': (1.0, 0.6),
     'L0_ffn_ln_b': (0.0, 0.775),
     'L0_ffn_b1': (0.0, 0.76),
     'L0_ffn_b2': (0.0, 0.534)}
    factors = {}
    for name, (base, spread) in spreads.items():
        noise = np.random.default_rng([zlib.crc32(name.encode()), seed]).standard_normal(out[name].shape)
        drawn = base * np.exp(spread * noise) if base else spread * noise
        out[name] = jnp.asarray(drawn.astype(out[name].dtype))
    for name, factor in factors.items():
        out[name] = (out[name] * factor).astype(out[name].dtype)
    return out
```

```python
from contextlib import ExitStack

import concourse.bass as bass
from concourse import mybir

P = 128
F32 = mybir.dt.float32
I32 = mybir.dt.int32
BF16 = mybir.dt.bfloat16
ALU = mybir.AluOpType
ACT = mybir.ActivationFunctionType
AX = mybir.AxisListType
ds = bass.ds

CHUNKS_PER_GROUP = 7
EPS = 1e-5


def gnn_moe(nc, x, src_t, dst_t, dst_first, wgt_t, w_nbr, w_own, bias, Wr, br, ln_g, ln_b, W1, b1, W2, b2, out):
    D = x.shape[1]
    NT = x.shape[0] // P
    N = 3125
    NROW = NT * P
    NCH = src_t.shape[1]
    CG = CHUNKS_PER_GROUP
    NG = NCH // CG
    NIT = NG // 2
    E = b1.shape[0]
    H = b1.shape[1]
    KD, KH = D // P, H // P
    MT = (2 * N + E * (P - 1)) // P
    TG = 5
    NTG = NT // TG
    AW = NROW + P
    TRASH = NROW
    assert NCH == 2 * NIT * CG and NT == TG * NTG and KD == 2 and MT % 2 == 0

    ctx = ExitStack()
    with ctx:
        def sb(name, cols, dt=F32, parts=P):
            return ctx.enter_context(nc.sbuf_tensor(name, [parts, cols], dt))

        def bank(name, n=1):
            return ctx.enter_context(nc.psum_tensor(name, [P, n, 512], F32))

        def sem(name):
            return ctx.enter_context(nc.semaphore(name))

        xn_dram = nc.dram_tensor("xn_dram", [NROW, D], F32).ap()
        ex_dram = nc.dram_tensor("ex_dram", [NROW + P, D], F32).ap()
        b1s_dram = nc.dram_tensor("b1s_dram", [3, E * H], BF16).ap()
        b2s_dram = nc.dram_tensor("b2s_dram", [3, E * D], BF16).ap()

        w1_sb = sb("w1_sb", E * KD * H)
        w2_sb = sb("w2_sb", E * KH * D)
        cut = [0]

        def early(cols):
            cut[0] += cols
            assert cut[0] <= E * KH * D
            return w2_sb[:, cut[0] - cols:cut[0]]

        agg_t = early(KD * AW)
        agg_v = agg_t.rearrange("p (k n) -> p k n", k=KD)
        xs = early(NT * D)
        wnbr_sb, wown_sb = early(KD * D), early(KD * D)
        xg_stage = early(TG * D)
        b1s_sb = sb("b1s_sb", E * H, BF16, 3)
        b2s_sb = sb("b2s_sb", E * D, BF16, 3)
        G = sb("G", 2 * CG * D)
        S = sb("S", 2 * CG * P)
        src_sb, dst_sb = sb("src_sb", NCH, I32), sb("dst_sb", NCH, I32)
        first_sb = sb("first_sb", NG, I32)
        wgt_sb = sb("wgt_sb", NCH)
        rel = sb("rel", NCH)
        rest = sb("rest", NCH)
        inside = sb("inside", NCH)
        idx_stage = sb("idx_stage", 2 * CG, I32)
        n_rest = sb("n_rest", 2)
        n_rest_i = sb("n_rest_i", 1, I32)
        ident, iota_f, ones, lower = sb("ident", P), sb("iota_f", P), sb("ones", P), sb("lower", P)
        ones3 = sb("ones3", P, BF16, 3)
        iota_e, iota_e8 = sb("iota_e", NT * E), sb("iota_e8", NT * E)
        node_id = sb("node_id", NT)
        trash_id = sb("trash_id", 1)
        eps_sb = sb("eps_sb", 1)
        bias_sb = sb("bias_sb", D)
        br_sb = sb("br_sb", E)
        wr_sb = sb("wr_sb", KD * E)
        lng_sb, lnb_sb = sb("lng_sb", KD * E), sb("lnb_sb", KD * E)
        stat = sb("stat", 2 * TG * 6)
        mv = sb("mv", NT * 2)
        rstd = sb("rstd", NT)
        mv2, rs2 = sb("mv2", 2 * TG * 2), sb("rs2", 2 * TG)
        nmr = sb("nmr", TG)
        one_tile = sb("one_tile", D)
        tile_t = sb("tile_t", TG * KD * P)
        zt, zn, z_t = G[:, 0:TG * D], G[:, TG * D:2 * TG * D], S[:, 0:TG * KD * P]
        logit = sb("logit", NT * E)
        small = [sb(f"small{i}", NT * E) for i in range(7)]
        per = [sb(f"per{i}", NT) for i in range(10)]
        slot_i = sb("slot_i", 2 * NT, I32)
        part_i = sb("part_i", 4 * NT, I32)
        place = sb("place", 4 * NT)
        per_e = [sb(f"per_e{i}", E) for i in range(6)]
        cnt_i = sb("cnt_i", 2 * E, I32)
        hot_row, hot_tile = sb("hot_row", 2 * P), sb("hot_tile", 2 * 2 * MT)
        tok = sb("tok", 2 * MT)
        slot_idx = sb("slot_idx", MT, I32)
        tile_e, tile_ei = sb("tile_e", MT), sb("tile_ei", MT, I32)
        gat_stage, sca_stage = sb("gat_stage", 2, I32), sb("sca_stage", 2, I32)
        hid, hid_t, xe, xe_t = G[:, 0:H], G[:, H:2 * H], G[:, 2 * H:2 * H + 2 * D], G[:, 2 * H + 2 * D:2 * H + 4 * D]
        y = sb("y", 2 * D)
        bpart = sb("bpart", 2 * (E * H // P))
        bsplit = sb("bsplit", 3 * (E * H // P), BF16)
        b2part = sb("b2part", 2 * (E * D // P))
        b2split = sb("b2split", 3 * (E * D // P), BF16)

        ps_agg = bank("ps_agg", 4)
        ps_t = bank("ps_t")
        ps_o = bank("ps_o")
        ps_l = bank("ps_l", 2)
        ps_h, ps_ht = ps_agg[:, 0:2, :], ps_agg[:, 2:4, :]

        x_in = [sem(f"x_in{g}") for g in range(NTG)]
        edges_in, small_in, w1_in, w2_in = sem("edges_in"), sem("small_in"), sem("w1_in"), sem("w2_in")
        parts_in, parts_out, parts_back = sem("parts_in"), sem("parts_out"), sem("parts_back")
        consts_ready, ones3_ready = sem("consts_ready"), sem("ones3_ready")
        dve_step, pool_step = sem("dve_step"), sem("pool_step")
        var_ready, std_ready = sem("var_ready"), sem("std_ready")
        xn_ready, xn_out = sem("xn_ready"), sem("xn_out")
        edge_tables, rest_summed, rest_ready = sem("edge_tables"), sem("rest_summed"), sem("rest_ready")
        gathered = [sem(f"gathered{k}") for k in range(2 * CG)]
        staged = sem("staged")
        s_ready, group_done, group_added = sem("s_ready"), sem("group_done"), sem("group_added")
        own_norm, own_tr, own_copied, own_done, own_added = (
            sem("own_norm"), sem("own_tr"), sem("own_copied"), sem("own_done"), sem("own_added"))
        r_gathered, r_staged, r_s, r_done, r_added, r_rel = (
            sem("r_gathered"), sem("r_staged"), sem("r_s"), sem("r_done"), sem("r_added"), sem("r_rel"))
        agg_copied, nbr_done, x1_ready, x1_out = sem("agg_copied"), sem("nbr_done"), sem("x1_ready"), sem("x1_out")
        var1, std1, z_ready, z_tr, z_copied, logit_done, logit_added = (
            sem("var1"), sem("std1"), sem("z_ready"), sem("z_tr"), sem("z_copied"), sem("logit_done"),
            sem("logit_added"))
        var2, std2, zn_scale, zn_ready, zn_out = sem("var2"), sem("std2"), sem("zn_scale"), sem("zn_ready"), sem("zn_out")
        carried, pool_carried = sem("carried"), sem("pool_carried")
        nbr_added, ng_step = sem("nbr_added"), sem("ng_step")
        trash_zero, trash_out = sem("trash_zero"), sem("trash_out")
        shifted, exp_ready, masks_ready, ranks_ready = (
            sem("shifted"), sem("exp_ready"), sem("masks_ready"), sem("ranks_ready"))
        hot_ready, hot_used, slots_ready = sem("hot_ready"), sem("hot_used"), sem("slots_ready")
        m_staged, m_sstaged = sem("m_staged"), sem("m_sstaged")
        m_gath = [sem(f"m_gath{k}") for k in range(2)]
        m_tr, m_xt, m_h, m_gelu, m_ht, m_htc, m_y, m_yw = (
            sem("m_tr"), sem("m_xt"), sem("m_h"), sem("m_gelu"), sem("m_ht"), sem("m_htc"), sem("m_y"), sem("m_yw"))
        m_sum = sem("m_sum")

        x_v = x.rearrange("(g t p) d -> g p t d", g=NTG, p=P)
        xn_v = xn_dram.rearrange("(g t p) d -> g p t d", g=NTG, p=P)

        block = ctx.enter_context(nc.Block())

        @block.sync
        def _(sp):
            for g in range(NTG):
                sp.dma_start(xs[:, g * TG * D:(g + 1) * TG * D].rearrange("p (t d) -> p t d", t=TG),
                             x_v[g]).then_inc(x_in[g], 16)
            sp.dma_start(wnbr_sb.rearrange("p (k n) -> p k n", k=KD),
                         w_nbr.rearrange("(k p) n -> p k n", p=P)).then_inc(small_in, 16)
            sp.dma_start(wown_sb.rearrange("p (k n) -> p k n", k=KD),
                         w_own.rearrange("(k p) n -> p k n", p=P)).then_inc(small_in, 16)
            sp.dma_start(bias_sb[:, :], bias.rearrange("(a n) -> a n", a=1).to_broadcast([P, D])
                         ).then_inc(small_in, 16)
            sp.dma_start(br_sb[:, :], br.rearrange("(a n) -> a n", a=1).to_broadcast([P, E])
                         ).then_inc(small_in, 16)
            sp.dma_start(wr_sb[:, :], Wr).then_inc(small_in, 16)
            sp.dma_start(lng_sb[:, :], ln_g).then_inc(small_in, 16)
            sp.dma_start(lnb_sb[:, :], ln_b).then_inc(small_in, 16)
            sp.dma_start(bpart[:, 0:E * H // P], b1.rearrange("e (q n) -> (e q) n", q=P // E)).then_inc(parts_in, 16)
            sp.dma_start(b2part[:, 0:E * D // P], b2.rearrange("e (q n) -> (e q) n", q=P // E)).then_inc(parts_in, 16)
            for g in range(NTG):
                sp.wait_ge(xn_ready, g + 1)
                sp.dma_start(xn_v[g], xg_stage.rearrange("p (t d) -> p t d", t=TG)).then_inc(xn_out, 16)
            for e in range(E):
                sp.dma_start(w1_sb[:, e * KD * H:(e + 1) * KD * H], W1[:, e, :]).then_inc(w1_in, 16)
            sp.wait_ge(trash_zero, 1)
            sp.dma_start(ex_dram[TRASH:TRASH + P, :], y[:, 0:D]).then_inc(trash_out, 16)
            sp.dma_start(out[TRASH:TRASH + P, :], y[:, 0:D]).then_inc(trash_out, 16)
            sp.wait_ge(parts_out, 6 * 16)
            sp.dma_start(b1s_sb[:, :], b1s_dram).then_inc(parts_back, 16)
            sp.dma_start(b2s_sb[:, :], b2s_dram).then_inc(parts_back, 16)
            with sp.Fori(0, NTG) as g:
                sp.wait_ge(x1_ready, g + 1)
                sp.dma_start(out[ds(g * (TG * P), TG * P), :].rearrange("(t p) d -> p t d", p=P),
                             xs[:, ds(g * (TG * D), TG * D)].rearrange("p (t d) -> p t d", t=TG)
                             ).then_inc(x1_out, 16)
                sp.wait_ge(zn_ready, g + 1)
                sp.dma_start(ex_dram[ds(g * (TG * P), TG * P), :].rearrange("(t p) d -> p t d", p=P),
                             zn[:, :].rearrange("p (t d) -> p t d", t=TG)).then_inc(zn_out, 16)
            sp.wait_ge(x1_out, 16 * NTG)
            sp.wait_ge(nbr_done, NT)
            for e in range(E):
                sp.dma_start(w2_sb[:, e * KH * D:(e + 1) * KH * D], W2[:, e, :]).then_inc(w2_in, 16)
            sp.wait_ge(trash_out, 32)

        @block.gpsimd
        def _(pool):
            n = 0
            for t, v in ((ident, 0.0), (lower, 1.0), (ones, 1.0), (eps_sb, EPS)):
                pool.memset(t[:, :], v).then_inc(pool_step, 1)
                n += 1
            pool.memset(y[:, 0:D], 0.0).then_inc(trash_zero, 1)
            pool.wait_ge(pool_step, n)
            pool.affine_select(out=ident[:, :], in_=ident[:, :], compare_op=ALU.not_equal, fill=1.0, base=0,
                               pattern=[[-1, P]], channel_multiplier=1).then_inc(consts_ready, 1)
            pool.affine_select(out=lower[:, :], in_=lower[:, :], compare_op=ALU.is_ge, fill=0.0, base=-1,
                               pattern=[[1, P]], channel_multiplier=-1).then_inc(consts_ready, 1)
            pool.iota(iota_f[:, :], [[1, P]], base=0, channel_multiplier=0,
                      allow_small_or_imprecise_dtypes=True).then_inc(consts_ready, 1)
            pool.iota(iota_e[:, :], [[0, NT], [1, E]], base=0, channel_multiplier=0,
                      allow_small_or_imprecise_dtypes=True).then_inc(consts_ready, 1)
            pool.iota(iota_e8[:, :], [[0, NT], [1, E]], base=E, channel_multiplier=0,
                      allow_small_or_imprecise_dtypes=True).then_inc(consts_ready, 1)
            pool.iota(node_id[:, :], [[P, NT]], base=1, channel_multiplier=1,
                      allow_small_or_imprecise_dtypes=True).then_inc(consts_ready, 1)
            pool.iota(trash_id[:, :], [[1, 1]], base=TRASH + 1, channel_multiplier=1,
                      allow_small_or_imprecise_dtypes=True).then_inc(consts_ready, 1)

            def gather(k, half, sems):
                pool.indirect_dma_start(
                    out=G[:, (half * CG + k) * D:(half * CG + k + 1) * D], out_offset=None, in_=xn_dram,
                    in_offset=bass.IndirectOffsetOnAxis(ap=idx_stage[:, half * CG + k:half * CG + k + 1], axis=0),
                ).then_inc(sems[k + half * CG], 16)

            pool.wait_ge(edges_in, 64)
            pool.wait_ge(xn_out, 16 * NTG)

            def fetch(i, first):
                for half in range(2):
                    if not first:
                        pool.wait_ge(group_done, 2 * i + half - 1)
                    pool.tensor_copy(idx_stage[:, half * CG:(half + 1) * CG],
                                     src_sb[:, ds(i * (2 * CG) + half * CG, CG)]).then_inc(staged, 1)
                    pool.wait_ge(staged, 2 * i + half + 1)
                    pool.sem_inc(pool_carried, 1)
                    for k in range(CG):
                        gather(k, half, gathered)

            fetch(0, True)
            with pool.Fori(1, NIT) as i:
                fetch(i, False)

            pool.wait_ge(rest_ready, 1)
            some = pool.value_load(n_rest_i[0:1, 0:1], min_val=0, max_val=1)
            pool.wait_ge(group_done, NG)
            with pool.If(some):
                with pool.Fori(0, NT) as w:
                    with pool.Fori(0, NG) as g:
                        pool.wait_ge(r_done, w * NG + g)
                        pool.tensor_copy(idx_stage[:, 0:CG], src_sb[:, ds(g * CG, CG)]).then_inc(r_staged, 1)
                        pool.wait_ge(r_staged, w * NG + g + 1)
                        pool.sem_inc(pool_carried, 1)
                        for k in range(CG):
                            pool.indirect_dma_start(
                                out=G[:, k * D:(k + 1) * D], out_offset=None, in_=xn_dram,
                                in_offset=bass.IndirectOffsetOnAxis(ap=idx_stage[:, k:k + 1], axis=0),
                            ).then_inc(gathered[k], 16)

            pool.wait_ge(slots_ready, 1)
            pool.wait_ge(zn_out, 16 * NTG)
            pool.wait_ge(trash_out, 32)
            pool.wait_ge(x1_out, 16 * NTG)

            def rows(i, first):
                if not first:
                    pool.wait_ge(m_tr, 2 * i)
                pool.tensor_copy(gat_stage[:, :], slot_idx[:, ds(i * 2, 2)]).then_inc(m_staged, 1)
                pool.wait_ge(m_staged, i + 1)
                pool.sem_inc(pool_carried, 1)
                for k in range(2):
                    pool.indirect_dma_start(
                        out=xe[:, k * D:(k + 1) * D], out_offset=None, in_=ex_dram,
                        in_offset=bass.IndirectOffsetOnAxis(ap=gat_stage[:, k:k + 1], axis=0),
                    ).then_inc(m_gath[k], 16)

            def add_rows(i, first):
                if not first:
                    pool.wait_ge(m_sum, 32 * i)
                pool.tensor_copy(sca_stage[:, :], slot_idx[:, ds(i * 2, 2)]).then_inc(m_sstaged, 1)
                pool.wait_ge(m_sstaged, i + 1)
                for k in range(2):
                    pool.wait_ge(m_yw, 2 * i + k + 1)
                    if k:
                        pool.wait_ge(m_sum, 32 * i + 16 * k)
                    pool.sem_inc(pool_carried, 1)
                    pool.indirect_dma_start(
                        out=out, out_offset=bass.IndirectOffsetOnAxis(ap=sca_stage[:, k:k + 1], axis=0),
                        in_=y[:, k * D:(k + 1) * D], in_offset=None, compute_op=ALU.add,
                    ).then_inc(m_sum, 16)

            rows(0, True)
            rows(1, False)
            add_rows(0, True)
            with pool.Fori(1, MT // 2 - 1) as i:
                rows(i + 1, False)
                add_rows(i, False)
            add_rows(MT // 2 - 1, False)
            pool.wait_ge(m_sum, 16 * MT)

        @block.vector
        def _(dve):
            steps = [0]

            def step(ins):
                steps[0] += 1
                ins.then_inc(dve_step, 1)
                dve.wait_ge(dve_step, steps[0])

            dve.memset(ones3[:, :], 1.0).then_inc(ones3_ready, 1)
            step(dve.memset(agg_t, 0.0))

            def moments(rows_of, stat_of, mv_of, n):
                for t in range(n):
                    last = dve.bn_stats(stat_of(t), rows_of(t))
                return last

            for g in range(NTG):
                dve.wait_ge(x_in[g], 16)
                for t in range(TG):
                    last = dve.bn_stats(stat[:, t * 6:t * 6 + 6], xs[:, (g * TG + t) * D:(g * TG + t + 1) * D])
                step(last)
                for t in range(TG):
                    last = dve.bn_aggr(mv[:, 2 * (g * TG + t):2 * (g * TG + t) + 2], stat[:, t * 6:t * 6 + 6])
                last.then_inc(var_ready, 1)
                dve.wait_ge(var_ready, g + 1)
                dve.wait_ge(std_ready, g + 1)
                step(dve.reciprocal(rstd[:, g * TG:(g + 1) * TG], rstd[:, g * TG:(g + 1) * TG]))
                if g:
                    dve.wait_ge(xn_out, 16 * g)
                for t in range(TG):
                    c = g * TG + t
                    last = dve.tensor_scalar(xg_stage[:, t * D:(t + 1) * D], xs[:, c * D:(c + 1) * D],
                                             mv[:, 2 * c:2 * c + 1], rstd[:, c:c + 1], ALU.subtract, ALU.mult)
                last.then_inc(xn_ready, 1)

            dve.wait_ge(edges_in, 64)
            step(dve.tensor_tensor(rel[:, :].rearrange("p (g k) -> p g k", k=CG),
                                   dst_sb[:, :].rearrange("p (g k) -> p g k", k=CG),
                                   first_sb[:, :].rearrange("p (g k) -> p g k", k=1).to_broadcast([P, NG, CG]),
                                   ALU.subtract))
            step(dve.tensor_scalar(inside[:, :], rel[:, :], 0.0, None, ALU.is_ge))
            step(dve.tensor_scalar(rest[:, :], rel[:, :], float(P), None, ALU.is_lt))
            step(dve.tensor_tensor(inside[:, :], inside[:, :], rest[:, :], ALU.mult))
            step(dve.scalar_tensor_tensor(out=rest[:, :], in0=inside[:, :], scalar=-8192.0, in1=dst_sb[:, :],
                                          op0=ALU.mult, op1=ALU.add))
            step(dve.tensor_reduce(n_rest[:, 0:1], inside[:, :], AX.X, ALU.add))
            dve.tensor_scalar(n_rest[:, 1:2], n_rest[:, 0:1], -1.0, float(NCH), ALU.mult, ALU.add
                              ).then_inc(edge_tables, 1)
            dve.wait_ge(rest_summed, 1)
            dve.tensor_scalar(n_rest_i[:, :], ps_l[:, 0, 0:1], 1.0, None, ALU.min).then_inc(rest_ready, 1)

            dve.wait_ge(parts_in, 32)
            for part, split, n in ((bpart, bsplit, E * H // P), (b2part, b2split, E * D // P)):
                a, b = part[:, 0:n], part[:, n:2 * n]
                step(dve.tensor_copy(split[:, 0:n], a))
                step(dve.tensor_tensor(b, a, split[:, 0:n], ALU.subtract))
                step(dve.tensor_copy(split[:, n:2 * n], b))
                step(dve.tensor_tensor(a, b, split[:, n:2 * n], ALU.subtract))
                dve.tensor_copy(split[:, 2 * n:3 * n], a).then_inc(parts_in, 1)

            dve.wait_ge(consts_ready, 7)
            dve.wait_ge(small_in, 7 * 16)

            def one_hots(table, c0, half, done):
                for k in range(CG):
                    s = half * CG + k
                    last = dve.tensor_scalar(S[:, s * P:(s + 1) * P], iota_f[:, :], table[:, ds(c0 + k, 1)],
                                             wgt_sb[:, ds(c0 + k, 1)], ALU.is_equal, ALU.mult)
                last.then_inc(done, 1)

            def sums(base, half, done):
                dve.tensor_tensor(agg_v[:, :, ds(base, P)], agg_v[:, :, ds(base, P)],
                                  ps_agg[:, 2 * half:2 * half + 2, 0:P], ALU.add).then_inc(done, 1)

            def own(t):
                if isinstance(t, int) and t == 0:
                    pass
                dve.tensor_scalar(one_tile[:, :], xs[:, ds(t * D, D)], mv[:, ds(2 * t, 1)], rstd[:, ds(t, 1)],
                                  ALU.subtract, ALU.mult).then_inc(own_norm, 1)

            def own_sum(t):
                dve.wait_ge(own_done, t + 1)
                dve.tensor_tensor(xs[:, ds(t * D, D)], xs[:, ds(t * D, D)], ps_o[:, 0, 0:D], ALU.add
                                  ).then_inc(own_added, 1)
                dve.wait_ge(own_added, 2 * t + 1)
                dve.tensor_tensor(xs[:, ds(t * D, D)], xs[:, ds(t * D, D)], bias_sb[:, :], ALU.add
                                  ).then_inc(own_added, 1)

            def add_group(i, half, g):
                base = dve.value_load(first_sb[0:1, ds(g, 1)], min_val=0, max_val=N - 1)
                dve.wait_ge(group_done, g + 1)
                if not (isinstance(g, int) and g == 0):
                    dve.wait_ge(group_added, g)
                sums(base, half, group_added)

            def groups(i, first, with_own):
                for half in range(2):
                    g = 2 * i + half
                    if not first:
                        dve.wait_ge(group_done, g - 1)
                    one_hots(rel, i * (2 * CG) + half * CG, half, s_ready)
                    if half == 0 and with_own:
                        own(i)
                    if half == 1:
                        add_group(i, 0, 2 * i)
                if with_own:
                    own_sum(i)
                add_group(i, 1, 2 * i + 1)

            groups(0, True, True)
            with dve.Fori(1, NT) as i:
                groups(i, False, True)
            with dve.Fori(NT, NIT) as i:
                groups(i, False, False)

            some = dve.value_load(n_rest_i[0:1, 0:1], min_val=0, max_val=1)
            with dve.If(some):
                with dve.Fori(0, NT) as w:
                    with dve.Fori(0, NG) as g:
                        dve.wait_ge(r_done, w * NG + g)
                        dve.wait_ge(r_rel, w)
                        one_hots(rest, g * CG, 0, r_s)
                        dve.wait_ge(r_done, w * NG + g + 1)
                        dve.wait_ge(r_added, w * NG + g)
                        sums(w * P, 0, r_added)
                    dve.tensor_scalar(rest[:, :], rest[:, :], float(-P), None, ALU.add).then_inc(r_rel, 1)

            def node_group(g):
                for k in range(TG):
                    dve.wait_ge(nbr_done, g * TG + k + 1)
                    at = xs[:, ds(g * (TG * D) + k * D, D)]
                    last = dve.tensor_tensor(at, at, ps_l[:, k % 2, 0:D], ALU.add)
                    last.then_inc(x1_ready, 1) if k == TG - 1 else last.then_inc(nbr_added, 1)
                dve.wait_ge(x1_ready, g + 1)
                dve.sem_inc(carried, 1)
                for k in range(TG):
                    last = dve.bn_stats(stat[:, 6 * k:6 * k + 6], xs[:, ds(g * (TG * D) + k * D, D)])
                last.then_inc(ng_step, 1)
                dve.wait_ge(ng_step, 4 * g + 1)
                dve.sem_inc(carried, 1)
                for k in range(TG):
                    last = dve.bn_aggr(mv2[:, 2 * k:2 * k + 2], stat[:, 6 * k:6 * k + 6])
                last.then_inc(var1, 1)
                dve.wait_ge(std1, g + 1)
                dve.reciprocal(rs2[:, 0:TG], rs2[:, 0:TG]).then_inc(ng_step, 1)
                dve.wait_ge(ng_step, 4 * g + 2)
                for k in range(TG):
                    last = dve.tensor_scalar(zt[:, k * D:(k + 1) * D], xs[:, ds(g * (TG * D) + k * D, D)],
                                             mv2[:, 2 * k:2 * k + 1], rs2[:, k:k + 1], ALU.subtract, ALU.mult)
                last.then_inc(z_ready, 1)
                dve.wait_ge(z_ready, g + 1)
                for k in range(TG):
                    last = dve.bn_stats(stat[:, 6 * (TG + k):6 * (TG + k) + 6], zt[:, k * D:(k + 1) * D])
                last.then_inc(ng_step, 1)
                dve.wait_ge(ng_step, 4 * g + 3)
                dve.sem_inc(carried, 1)
                for k in range(TG):
                    last = dve.bn_aggr(mv2[:, 2 * (TG + k):2 * (TG + k) + 2], stat[:, 6 * (TG + k):6 * (TG + k) + 6])
                last.then_inc(var2, 1)
                dve.wait_ge(std2, g + 1)
                dve.reciprocal(rs2[:, TG:2 * TG], rs2[:, TG:2 * TG]).then_inc(ng_step, 1)
                dve.wait_ge(ng_step, 4 * g + 4)
                dve.scalar_tensor_tensor(out=nmr[:, :], in0=mv2[:, 2 * TG:4 * TG:2], scalar=-1.0,
                                         in1=rs2[:, TG:2 * TG], op0=ALU.mult, op1=ALU.mult).then_inc(zn_scale, 1)
                dve.wait_ge(logit_done, g + 1)
                dve.tensor_tensor(logit[:, ds(g * (TG * E), TG * E)].rearrange("p (t e) -> p t e", e=E),
                                  ps_o[:, 0, 0:TG * E].rearrange("p (t e) -> p t e", e=E),
                                  br_sb[:, :].rearrange("p (t e) -> p t e", t=1).to_broadcast([P, TG, E]),
                                  ALU.add).then_inc(logit_added, 1)

            with dve.Fori(0, NTG) as g:
                node_group(g)

            def te(t):
                return t[:, :].rearrange("p (t e) -> p t e", e=E)

            def over_e(v):
                return v[:, :].rearrange("p (t a) -> p t a", a=1).to_broadcast([P, NT, E])

            pr, m1, m2, a, b, c, sl = small
            mx, sm, p1, i1, p2, i2, valid, tokv, w1v, w2v = per
            dve.wait_ge(logit_added, NTG)
            step(dve.tensor_reduce(mx[:, :], te(logit), AX.X, ALU.max))
            dve.tensor_tensor(te(a), te(logit), over_e(mx), ALU.subtract).then_inc(shifted, 1)
            dve.tensor_scalar(valid[:, :], node_id[:, :], float(N), None, ALU.is_le)
            dve.wait_ge(exp_ready, 1)
            step(dve.tensor_reduce(sm[:, :], te(b), AX.X, ALU.add))
            step(dve.reciprocal(sm[:, :], sm[:, :]))
            step(dve.tensor_tensor(te(pr), te(b), over_e(sm), ALU.mult))
            for mask, best, at in ((m1, p1, i1), (m2, p2, i2)):
                step(dve.tensor_reduce(best[:, :], te(pr), AX.X, ALU.max))
                step(dve.tensor_tensor(te(a), te(pr), over_e(best), ALU.is_equal))
                step(dve.scalar_tensor_tensor(out=b[:, :], in0=a[:, :], scalar=float(-E), in1=iota_e8[:, :],
                                              op0=ALU.mult, op1=ALU.add))
                step(dve.tensor_reduce(at[:, :], te(b), AX.X, ALU.min))
                step(dve.tensor_tensor(te(mask), te(iota_e), over_e(at), ALU.is_equal))
                if mask is m1:
                    step(dve.scalar_tensor_tensor(out=pr[:, :], in0=mask[:, :], scalar=-2.0, in1=pr[:, :],
                                                  op0=ALU.mult, op1=ALU.add))
            step(dve.tensor_tensor(te(m1), te(m1), over_e(valid), ALU.mult))
            step(dve.tensor_tensor(te(m2), te(m2), over_e(valid), ALU.mult))
            dve.tensor_tensor(a[:, :].rearrange("p (e t) -> p t e", e=E), te(m1), te(m2), ALU.add
                              ).then_inc(masks_ready, 1)
            step(dve.tensor_tensor(sm[:, :], p1[:, :], p2[:, :], ALU.add))
            step(dve.reciprocal(sm[:, :], sm[:, :]))
            step(dve.tensor_tensor(sm[:, :], sm[:, :], valid[:, :], ALU.mult))
            dve.tensor_tensor(w1v[:, :], p1[:, :], sm[:, :], ALU.mult)
            dve.tensor_tensor(w2v[:, :], p2[:, :], sm[:, :], ALU.mult)
            step(dve.tensor_tensor(tokv[:, :], node_id[:, :], valid[:, :], ALU.mult))

            dve.wait_ge(ranks_ready, 1)
            step(dve.tensor_copy(b[:, :], ps_l[:, 1, 0:NT * E]))
            step(dve.memset(c[:, :], 1.0))
            step(dve.tensor_tensor_scan(sl[:, :], c[:, :], b[:, :], 0.0, ALU.mult, ALU.add))
            cnt, start, tiles, upto, tbase, off = per_e
            sl_e = sl[:, :].rearrange("p (e t) -> p e t", e=E)
            step(dve.tensor_tensor(b[:, :], sl[:, :], b[:, :], ALU.subtract))
            b_e = b[:, :].rearrange("p (e t) -> p e t", e=E)
            step(dve.tensor_copy(start[:, :], b_e[:, :, 0]))
            step(dve.tensor_tensor(cnt[:, :], sl_e[:, :, NT - 1], start[:, :], ALU.subtract))
            step(dve.tensor_scalar(cnt_i[:, 0:E], cnt[:, :], float(P - 1), None, ALU.add))
            step(dve.tensor_scalar(cnt_i[:, E:2 * E], cnt_i[:, 0:E], 7, None, ALU.arith_shift_right))
            step(dve.tensor_copy(tiles[:, :], cnt_i[:, E:2 * E]))
            step(dve.tensor_tensor_scan(upto[:, :], c[:, 0:E], tiles[:, :], 0.0, ALU.mult, ALU.add))
            step(dve.tensor_tensor(tbase[:, :], upto[:, :], tiles[:, :], ALU.subtract))
            step(dve.scalar_tensor_tensor(out=off[:, :], in0=tbase[:, :], scalar=float(P), in1=start[:, :],
                                          op0=ALU.mult, op1=ALU.subtract))
            step(dve.tensor_tensor(b[:, :], b[:, :], ps_l[:, 0, 0:NT * E], ALU.add))
            step(dve.tensor_tensor(te(sl), b[:, :].rearrange("p (e t) -> p t e", e=E),
                                   off[:, :].rearrange("p (a e) -> p a e", a=1).to_broadcast([P, NT, E]), ALU.add))
            for k, mask in enumerate((m1, m2)):
                step(dve.tensor_tensor(te(a), te(mask), te(sl), ALU.mult))
                step(dve.tensor_reduce(mx[:, :], te(a), AX.X, ALU.add))
                step(dve.tensor_copy(slot_i[:, k * NT:(k + 1) * NT], mx[:, :]))
                at = slot_i[:, k * NT:(k + 1) * NT]
                dve.tensor_scalar(part_i[:, 2 * k * NT:(2 * k + 1) * NT], at, 7, None, ALU.arith_shift_right)
                step(dve.tensor_scalar(part_i[:, (2 * k + 1) * NT:(2 * k + 2) * NT], at, P - 1, None, ALU.bitwise_and))
            step(dve.tensor_copy(place[:, :], part_i[:, :]))

            step(dve.tensor_scalar(tile_e[:, :], iota_f[:, 0:MT], tbase[:, 1:2], None, ALU.is_ge))
            for e in range(2, E):
                step(dve.scalar_tensor_tensor(out=tile_e[:, :], in0=iota_f[:, 0:MT], scalar=tbase[:, e:e + 1],
                                              in1=tile_e[:, :], op0=ALU.is_ge, op1=ALU.add))
            step(dve.tensor_copy(tile_ei[:, :], tile_e[:, :]))

            def slots_of(t, first):
                for k, wv in enumerate((w1v, w2v)):
                    if not first:
                        dve.wait_ge(hot_used, 2 * t + k - 1)
                    o = k * 2 * MT
                    dve.tensor_scalar(hot_row[:, k * P:(k + 1) * P], iota_f[:, :],
                                      place[:, ds((2 * k + 1) * NT + t, 1)], None, ALU.is_equal)
                    dve.tensor_scalar(hot_tile[:, o:o + MT], iota_f[:, 0:MT], place[:, ds(2 * k * NT + t, 1)],
                                      tokv[:, ds(t, 1)], ALU.is_equal, ALU.mult)
                    dve.tensor_scalar(hot_tile[:, o + MT:o + 2 * MT], iota_f[:, 0:MT],
                                      place[:, ds(2 * k * NT + t, 1)], wv[:, ds(t, 1)], ALU.is_equal, ALU.mult
                                      ).then_inc(hot_ready, 1)

            slots_of(0, True)
            with dve.Fori(1, NT) as t:
                slots_of(t, False)
            dve.wait_ge(hot_used, 2 * NT)
            step(dve.tensor_copy(tok[:, :], ps_o[:, 0, 0:2 * MT]))
            step(dve.tensor_scalar(tile_e[:, :], tok[:, 0:MT], 0.0, trash_id[:, :], ALU.is_equal, ALU.mult))
            step(dve.scalar_tensor_tensor(out=tile_e[:, :], in0=tile_e[:, :], scalar=-1.0, in1=tok[:, 0:MT],
                                          op0=ALU.add, op1=ALU.add))
            dve.tensor_copy(slot_idx[:, :], tile_e[:, :]).then_inc(slots_ready, 1)

            def hidden_copy(a):
                for n in range(2):
                    dve.wait_ge(m_ht, 2 * a + n + 1)
                    if n == 0 and not (isinstance(a, int) and a == 0):
                        dve.wait_ge(m_y, a)
                    dve.tensor_copy(hid_t[:, n * 512:(n + 1) * 512], ps_ht[:, n, :]).then_inc(m_htc, 1)

            def weigh(a, k):
                dve.wait_ge(m_y, a + 1)
                if not (isinstance(a, int) and a < 2):
                    dve.wait_ge(m_sum, 16 * a - 16)
                dve.tensor_scalar(y[:, k * D:(k + 1) * D], ps_o[:, 0, 0:D], tok[:, ds(a + MT, 1)], None, ALU.mult
                                  ).then_inc(m_yw, 1)

            dve.wait_ge(trash_out, 32)
            hidden_copy(0)
            weigh(0, 0)
            hidden_copy(1)
            weigh(1, 1)
            with dve.Fori(1, MT // 2) as i:
                for k in range(2):
                    hidden_copy(2 * i + k)
                    weigh(2 * i + k, k)

        @block.scalar
        def _(act):
            act.dma_start(src_sb[:, :], src_t).then_inc(edges_in, 16)
            act.dma_start(dst_sb[:, :], dst_t).then_inc(edges_in, 16)
            act.dma_start(wgt_sb[:, :], wgt_t).then_inc(edges_in, 16)
            act.dma_start(first_sb[:, :], dst_first.to_broadcast([P, NG])).then_inc(edges_in, 16)
            act.wait_ge(consts_ready, 1)
            for g in range(NTG):
                act.wait_ge(var_ready, g + 1)
                v = mv[:, 2 * g * TG:2 * (g + 1) * TG]
                act.activation(rstd[:, g * TG:(g + 1) * TG], v[:, 1:2 * TG:2], ACT.Sqrt, bias=eps_sb[:, :]
                               ).then_inc(std_ready, 1)
            act.wait_ge(parts_in, 34)
            for split, dram, n in ((bsplit, b1s_dram, E * H // P), (b2split, b2s_dram, E * D // P)):
                for j in range(3):
                    act.dma_start(dram[j:j + 1, :].rearrange("a (p n) -> (a p) n", p=P),
                                  split[:, j * n:(j + 1) * n]).then_inc(parts_out, 16)

            with act.Fori(0, NT) as t:
                act.wait_ge(own_tr, t + 1)
                act.activation(tile_t[:, 0:KD * P], ps_t[:, 0, 0:KD * P], ACT.Copy).then_inc(own_copied, 1)

            some = act.value_load(n_rest_i[0:1, 0:1], min_val=0, max_val=1)
            act.wait_ge(group_added, NG)
            with act.If(some):
                act.wait_ge(r_added, NT * NG)

            def node_group(g, first):
                for k in range(TG):
                    if not first:
                        act.wait_ge(nbr_done, g * TG + k - TG + 1)
                    act.activation(tile_t[:, k * KD * P:(k + 1) * KD * P].rearrange("p (k n) -> p k n", k=KD),
                                   agg_v[:, :, ds(g * (TG * P) + k * P, P)], ACT.Copy).then_inc(agg_copied, 1)
                act.wait_ge(var1, g + 1)
                act.activation(rs2[:, 0:TG], mv2[:, 1:2 * TG:2], ACT.Sqrt, bias=eps_sb[:, :]).then_inc(std1, 1)
                for k in range(TG):
                    act.wait_ge(z_tr, g * TG + k + 1)
                    act.activation(z_t[:, k * KD * P:(k + 1) * KD * P], ps_t[:, 0, 0:KD * P], ACT.Copy
                                   ).then_inc(z_copied, 1)
                act.wait_ge(var2, g + 1)
                act.activation(rs2[:, TG:2 * TG], mv2[:, 2 * TG + 1:4 * TG:2], ACT.Sqrt, bias=eps_sb[:, :]
                               ).then_inc(std2, 1)
                act.wait_ge(zn_scale, g + 1)
                if not first:
                    act.wait_ge(zn_out, 16 * g)
                for k in range(TG):
                    last = act.activation(zn[:, k * D:(k + 1) * D], zt[:, k * D:(k + 1) * D], ACT.Identity,
                                          bias=nmr[:, k:k + 1], scale=rs2[:, TG + k:TG + k + 1])
                last.then_inc(zn_ready, 1)

            act.wait_ge(own_done, NT)
            node_group(0, True)
            with act.Fori(1, NTG) as g:
                node_group(g, False)

            act.wait_ge(shifted, 1)
            act.activation(small[4][:, :], small[3][:, :], ACT.Exp).then_inc(exp_ready, 1)

            act.wait_ge(slots_ready, 1)

            def scaled(a, k):
                e = act.value_load(tile_ei[0:1, ds(a, 1)], min_val=0, max_val=E - 1)
                act.wait_ge(m_tr, a + 1)
                if not (isinstance(a, int) and a < 2):
                    act.wait_ge(m_h, 2 * a - 2)
                for d in range(KD):
                    last = act.activation(xe_t[:, (k * KD + d) * P:(k * KD + d + 1) * P],
                                          ps_t[:, 0, d * P:(d + 1) * P], ACT.Identity,
                                          bias=lnb_sb[:, ds(e + d * E, 1)], scale=lng_sb[:, ds(e + d * E, 1)])
                last.then_inc(m_xt, 1)

            def gelu(a):
                for n in range(2):
                    act.wait_ge(m_h, 2 * a + n + 1)
                    if n == 0 and not (isinstance(a, int) and a == 0):
                        act.wait_ge(m_ht, 2 * a)
                    act.activation(hid[:, n * 512:(n + 1) * 512], ps_h[:, n, :], ACT.Gelu).then_inc(m_gelu, 1)

            scaled(0, 0)
            scaled(1, 1)
            gelu(0)
            with act.Fori(1, MT // 2) as i:
                scaled(2 * i, 0)
                gelu(2 * i - 1)
                scaled(2 * i + 1, 1)
                gelu(2 * i)
            gelu(MT - 1)

        @block.tensor
        def _(pe):
            pe.wait_ge(edge_tables, 1)
            pe.wait_ge(consts_ready, 7)
            pe.matmul(ps_l[:, 0, 0:1], ones[:, :], n_rest[:, 1:2], start=True, stop=True).then_inc(rest_summed, 1)
            pe.wait_ge(small_in, 7 * 16)

            def products(half, count, ready, done, waits):
                for k in range(CG):
                    s = half * CG + k
                    pe.wait_ge(gathered[s], count)
                    if k == 0:
                        waits()
                    for d in range(KD):
                        last = pe.matmul(ps_agg[:, 2 * half + d, 0:P], G[:, s * D + d * P:s * D + (d + 1) * P],
                                         S[:, s * P:(s + 1) * P], start=(k == 0), stop=(k == CG - 1))
                last.then_inc(done, 1)

            def group(i, half, first):
                def waits():
                    pe.wait_ge(s_ready, 2 * i + half + 1)
                    if not first:
                        pe.wait_ge(group_added, 2 * i + half - 1)
                products(half, 16 * i + 16, s_ready, group_done, waits)

            def own_transpose(t, first):
                pe.wait_ge(own_norm, t + 1)
                if not first:
                    pe.wait_ge(own_copied, t)
                for d in range(KD):
                    last = pe.transpose(ps_t[:, 0, d * P:(d + 1) * P], one_tile[:, d * P:(d + 1) * P], ident[:, :])
                last.then_inc(own_tr, 1)

            def own_product(t, first):
                pe.wait_ge(own_copied, t + 1)
                if not first:
                    pe.wait_ge(own_added, 2 * t - 1)
                for d in range(KD):
                    last = pe.matmul(ps_o[:, 0, 0:D], tile_t[:, d * P:(d + 1) * P], wown_sb[:, d * D:(d + 1) * D],
                                     start=(d == 0), stop=(d == KD - 1))
                last.then_inc(own_done, 1)

            def iteration(i, first, with_own):
                if with_own:
                    own_transpose(i, first)
                group(i, 0, first)
                if with_own:
                    own_product(i, first)
                group(i, 1, first)

            iteration(0, True, True)
            with pe.Fori(1, NT) as i:
                iteration(i, False, True)
            with pe.Fori(NT, NIT) as i:
                iteration(i, False, False)

            pe.wait_ge(rest_ready, 1)
            pe.wait_ge(group_added, NG)
            some = pe.value_load(n_rest_i[0:1, 0:1], min_val=0, max_val=1)
            with pe.If(some):
                with pe.Fori(0, NT) as w:
                    with pe.Fori(0, NG) as g:
                        def waits():
                            pe.wait_ge(r_s, w * NG + g + 1)
                            pe.wait_ge(r_added, w * NG + g)
                        products(0, w * (16 * NG) + g * 16 + 16 + 16 * NIT, r_s, r_done, waits)

            def node_group(g, first):
                for k in range(TG):
                    pe.wait_ge(agg_copied, g * TG + k + 1)
                    if k >= 2:
                        pe.wait_ge(nbr_added, g * (TG - 1) + k - 1)
                    elif not first:
                        pe.wait_ge(x1_ready, g)
                    for d in range(KD):
                        last = pe.matmul(ps_l[:, k % 2, 0:D], tile_t[:, (k * KD + d) * P:(k * KD + d + 1) * P],
                                         wnbr_sb[:, d * D:(d + 1) * D], start=(d == 0), stop=(d == KD - 1))
                    last.then_inc(nbr_done, 1)
                pe.wait_ge(z_ready, g + 1)
                for k in range(TG):
                    if not (first and k == 0):
                        pe.wait_ge(z_copied, g * TG + k)
                    for d in range(KD):
                        last = pe.transpose(ps_t[:, 0, d * P:(d + 1) * P], zt[:, k * D + d * P:k * D + (d + 1) * P],
                                            ident[:, :])
                    last.then_inc(z_tr, 1)
                if not first:
                    pe.wait_ge(logit_added, g)
                for k in range(TG):
                    pe.wait_ge(z_copied, g * TG + k + 1)
                    for d in range(KD):
                        last = pe.matmul(ps_o[:, 0, k * E:(k + 1) * E], z_t[:, (k * KD + d) * P:(k * KD + d + 1) * P],
                                         wr_sb[:, d * E:(d + 1) * E], start=(d == 0), stop=(d == KD - 1))
                last.then_inc(logit_done, 1)

            pe.wait_ge(own_added, 2 * NT)
            node_group(0, True)
            with pe.Fori(1, NTG) as g:
                node_group(g, False)

            pe.wait_ge(masks_ready, 1)
            pe.matmul(ps_l[:, 0, 0:NT * E], lower[:, :], small[3][:, :], start=True, stop=True)
            pe.matmul(ps_l[:, 1, 0:NT * E], ones[:, :], small[3][:, :], start=True, stop=True).then_inc(ranks_ready, 1)

            def slots_of(t, first, final):
                for k in range(2):
                    pe.wait_ge(hot_ready, 2 * t + k + 1)
                    pe.matmul(ps_o[:, 0, 0:2 * MT], hot_row[:, k * P:(k + 1) * P],
                              hot_tile[:, k * 2 * MT:(k + 1) * 2 * MT], start=(first and k == 0),
                              stop=(final and k == 1), skip_group_check=True).then_inc(hot_used, 1)

            pe.wait_ge(logit_added, NTG)
            slots_of(0, True, False)
            with pe.Fori(1, NT - 1) as t:
                slots_of(t, False, False)
            slots_of(NT - 1, False, True)

            pe.wait_ge(slots_ready, 1)
            pe.wait_ge(w1_in, 16 * E)
            pe.wait_ge(w2_in, 16 * E)
            pe.wait_ge(parts_back, 32)
            pe.wait_ge(ones3_ready, 1)

            def expert(a):
                return pe.value_load(tile_ei[0:1, ds(a, 1)], min_val=0, max_val=E - 1)

            def rows_t(a, k, n):
                pe.wait_ge(m_gath[k], n)
                if not (isinstance(a, int) and a == 0):
                    pe.wait_ge(m_xt, a)
                for d in range(KD):
                    last = pe.transpose(ps_t[:, 0, d * P:(d + 1) * P], xe[:, k * D + d * P:k * D + (d + 1) * P],
                                        ident[:, :])
                last.then_inc(m_tr, 1)

            def layer1(a, k, e):
                pe.wait_ge(m_xt, a + 1)
                for n in range(2):
                    if not (isinstance(a, int) and a == 0):
                        pe.wait_ge(m_gelu, 2 * a - 1 + n)
                    pe.matmul(ps_h[:, n, :], ones3[:, :], b1s_sb[:, ds(e * H + n * 512, 512)], start=True, stop=False)
                    for d in range(KD):
                        last = pe.matmul(ps_h[:, n, :], xe_t[:, (k * KD + d) * P:(k * KD + d + 1) * P],
                                         w1_sb[:, ds(e * (KD * H) + d * H + n * 512, 512)],
                                         start=False, stop=(d == KD - 1))
                    last.then_inc(m_h, 1)

            def layer2(a, e):
                if not (isinstance(a, int) and a == 0):
                    pe.wait_ge(m_yw, a)
                pe.matmul(ps_o[:, 0, 0:D], ones3[:, :], b2s_sb[:, ds(e * D, D)], start=True, stop=False)
                for j in range(KH):
                    if j % 4 == 0:
                        pe.wait_ge(m_htc, 2 * a + j // 4 + 1)
                    last = pe.matmul(ps_o[:, 0, 0:D], hid_t[:, j * P:(j + 1) * P],
                                     w2_sb[:, ds(e * (KH * D) + j * D, D)], start=False, stop=(j == KH - 1))
                last.then_inc(m_y, 1)

            def hidden_t(a):
                for n in range(2):
                    pe.wait_ge(m_gelu, 2 * a + n + 1)
                    if not (isinstance(a, int) and a == 0):
                        pe.wait_ge(m_htc, 2 * a - 1 + n)
                    for j in range(4):
                        last = pe.transpose(ps_ht[:, n, j * P:(j + 1) * P],
                                            hid[:, (4 * n + j) * P:(4 * n + j + 1) * P], ident[:, :])
                    last.then_inc(m_ht, 1)

            rows_t(0, 0, 16)
            rows_t(1, 1, 16)
            layer1(0, 0, expert(0))
            hidden_t(0)
            with pe.Fori(1, MT // 2) as i:
                rows_t(2 * i, 0, 16 * i + 16)
                layer1(2 * i - 1, 1, expert(2 * i - 1))
                layer2(2 * i - 2, expert(2 * i - 2))
                hidden_t(2 * i - 1)
                rows_t(2 * i + 1, 1, 16 * i + 16)
                layer1(2 * i, 0, expert(2 * i))
                layer2(2 * i - 1, expert(2 * i - 1))
                hidden_t(2 * i)
            layer1(MT - 1, 1, expert(MT - 1))
            layer2(MT - 2, expert(MT - 2))
            hidden_t(MT - 1)
            layer2(MT - 1, expert(MT - 1))


def kernel(x, src, dst, edge_weight, L0_gnn_w_nbr, L0_gnn_w_own, L0_gnn_bias, L0_ffn_Wr, L0_ffn_br, L0_ffn_ln_g,
           L0_ffn_ln_b, L0_ffn_W1, L0_ffn_b1, L0_ffn_W2, L0_ffn_b2):
    import numpy as np
    import concourse.bacc as bacc
    from concourse.bass_utils import run_bass_kernel_spmd

    n, d = x.shape
    rows = -(-n // P) * P
    per_it = 2 * CHUNKS_PER_GROUP * P
    edges = -(-len(src) // per_it) * per_it
    experts, _, hidden = L0_ffn_W1.shape

    def chunks(v, mode="constant"):
        return np.pad(np.asarray(v), (0, edges - len(v)), mode=mode).reshape(-1, P)

    dst_c = chunks(dst, "edge")
    arrays = {
        "x": np.pad(np.asarray(x), ((0, rows - n), (0, 0))),
        "src_t": np.ascontiguousarray(chunks(src).T),
        "dst_t": np.ascontiguousarray(dst_c.T),
        "dst_first": np.ascontiguousarray(dst_c[::CHUNKS_PER_GROUP, 0].reshape(1, -1)),
        "wgt_t": np.ascontiguousarray(chunks(edge_weight).T),
        "w_nbr": np.asarray(L0_gnn_w_nbr), "w_own": np.asarray(L0_gnn_w_own), "bias": np.asarray(L0_gnn_bias),
        "Wr": np.ascontiguousarray(np.asarray(L0_ffn_Wr).reshape(-1, P, experts).transpose(1, 0, 2).reshape(P, -1)),
        "br": np.asarray(L0_ffn_br),
        "ln_g": np.ascontiguousarray(np.asarray(L0_ffn_ln_g).reshape(experts, -1, P).transpose(2, 1, 0).reshape(P, -1)),
        "ln_b": np.ascontiguousarray(np.asarray(L0_ffn_ln_b).reshape(experts, -1, P).transpose(2, 1, 0).reshape(P, -1)),
        "W1": np.ascontiguousarray(np.asarray(L0_ffn_W1).reshape(experts, -1, P, hidden).transpose(2, 0, 1, 3)
                                   .reshape(P, experts, -1)),
        "b1": np.asarray(L0_ffn_b1),
        "W2": np.ascontiguousarray(np.asarray(L0_ffn_W2).reshape(experts, -1, P, d).transpose(2, 0, 1, 3)
                                   .reshape(P, experts, -1)),
        "b2": np.asarray(L0_ffn_b2),
    }
    nc = bacc.Bacc("TRN2", target_bir_lowering=False, num_devices=1)
    args = [nc.dram_tensor(k, v.shape, mybir.dt.from_np(v.dtype), kind="ExternalInput").ap()
            for k, v in arrays.items()]
    out = nc.dram_tensor("out", (rows + P, d), F32, kind="ExternalOutput").ap()
    gnn_moe(nc, *args, out)
    r = run_bass_kernel_spmd(nc, [arrays], core_ids=[0])
    return r.results[0]["out"][:n]
```

```python
from contextlib import ExitStack

import concourse.bass as bass
from concourse import mybir

P = 128
F32 = mybir.dt.float32
I32 = mybir.dt.int32
BF16 = mybir.dt.bfloat16
ALU = mybir.AluOpType
ACT = mybir.ActivationFunctionType
AX = mybir.AxisListType
ds = bass.ds

CHUNKS_PER_GROUP = 7
LAG = 5
EPS = 1e-5


def gnn_moe(nc, x, src_t, dst_t, dst_first, wgt_t, w_nbr, w_own, bias, Wr, br, ln_g, ln_b, W1, b1, W2, b2, out):
    D = x.shape[1]
    NT = x.shape[0] // P
    N = 3125
    NROW = NT * P
    NCH = src_t.shape[1]
    CG = CHUNKS_PER_GROUP
    NG = NCH // CG
    NIT = NG // 2
    E = b1.shape[0]
    H = b1.shape[1]
    KD, KH = D // P, H // P
    MT = (2 * N + E * (P - 1)) // P
    TG = 5
    NTG = NT // TG
    AW = NROW + P
    TRASH = NROW
    assert NCH == 2 * NIT * CG and NT == TG * NTG and KD == 2 and MT % 4 == 0
    assert LAG + 2 < NIT < NT + LAG

    ctx = ExitStack()
    with ctx:
        def sb(name, cols, dt=F32, parts=P):
            return ctx.enter_context(nc.sbuf_tensor(name, [parts, cols], dt))

        def bank(name, n=1):
            return ctx.enter_context(nc.psum_tensor(name, [P, n, 512], F32))

        def sem(name):
            return ctx.enter_context(nc.semaphore(name))

        xn_dram = nc.dram_tensor("xn_dram", [NROW, D], F32).ap()
        ex_dram = nc.dram_tensor("ex_dram", [NROW + P, D], F32).ap()
        b1s_dram = nc.dram_tensor("b1s_dram", [3, E * H], BF16).ap()
        b2s_dram = nc.dram_tensor("b2s_dram", [3, E * D], BF16).ap()

        w1_sb = sb("w1_sb", E * KD * H)
        w2_sb = sb("w2_sb", E * KH * D)
        cut = [0]

        def early(cols):
            cut[0] += cols
            assert cut[0] <= E * KH * D
            return w2_sb[:, cut[0] - cols:cut[0]]

        agg_t = early(KD * AW)
        agg_v = agg_t.rearrange("p (k n) -> p k n", k=KD)
        xs = early(NT * D)
        wnbr_sb, wown_sb = early(KD * D), early(KD * D)
        xg_stage = early(TG * D)
        b1s_sb = sb("b1s_sb", E * H, BF16, 3)
        b2s_sb = sb("b2s_sb", E * D, BF16, 3)
        G = sb("G", 2 * CG * D)
        S = sb("S", 2 * CG * P)
        dst_sb = sb("dst_sb", NCH, I32)
        first_sb = sb("first_sb", NG, I32)
        wgt_sb = sb("wgt_sb", NCH)
        rel = sb("rel", NCH)
        rest = sb("rest", NCH)
        inside = sb("inside", NCH)
        early_g = sb("early_g", 2 * NG)
        idx_stage, r_stage = sb("idx_stage", 2 * CG, I32), sb("r_stage", CG, I32)
        n_bad = sb("n_bad", 3)
        good = sb("good", 1)
        bad_i = sb("bad_i", 1, I32)
        ident, iota_f, ones, lower = sb("ident", P), sb("iota_f", P), sb("ones", P), sb("lower", P)
        ones3 = sb("ones3", P, BF16, 3)
        iota_e, iota_e8 = sb("iota_e", NT * E), sb("iota_e8", NT * E)
        node_id = sb("node_id", NT)
        trash_id = sb("trash_id", 1)
        eps_sb = sb("eps_sb", 1)
        bias_sb = sb("bias_sb", D)
        br_sb = sb("br_sb", E)
        wr_sb = sb("wr_sb", KD * E)
        lng_sb, lnb_sb = sb("lng_sb", KD * E), sb("lnb_sb", KD * E)
        stat = sb("stat", 2 * TG * 6)
        mv = sb("mv", NT * 2)
        rstd = sb("rstd", NT)
        mv2, rs2 = sb("mv2", 4), sb("rs2", 2)
        nmr = sb("nmr", 1)
        one_tile = sb("one_tile", D)
        tile_t = sb("tile_t", 2 * KD * P)
        zt, zn, z_t = sb("zt", D), sb("zn", D), sb("z_t", KD * P)
        logit = sb("logit", NT * E)
        small = [sb(f"small{i}", NT * E) for i in range(7)]
        per = [sb(f"per{i}", NT) for i in range(10)]
        slot_i = sb("slot_i", 2 * NT, I32)
        part_i = sb("part_i", 4 * NT, I32)
        place = sb("place", 4 * NT)
        per_e = [sb(f"per_e{i}", E) for i in range(6)]
        cnt_i = sb("cnt_i", 2 * E, I32)
        hot_row, hot_tile = sb("hot_row", 2 * P), sb("hot_tile", 2 * 2 * MT)
        tok = sb("tok", 2 * MT)
        slot_idx = sb("slot_idx", MT, I32)
        tile_e, tile_ei = sb("tile_e", MT), sb("tile_ei", MT, I32)
        gat_stage, sca_stage = sb("gat_stage", 4, I32), sb("sca_stage", 2, I32)
        hid, hid_t, xe, xe_t = G[:, 0:H], G[:, H:2 * H], G[:, 2 * H:2 * H + 4 * D], G[:, 2 * H + 4 * D:2 * H + 6 * D]
        y = sb("y", 2 * D)
        bpart = sb("bpart", 2 * (E * H // P))
        bsplit = sb("bsplit", 3 * (E * H // P), BF16)
        b2part = sb("b2part", 2 * (E * D // P))
        b2split = sb("b2split", 3 * (E * D // P), BF16)

        ps_agg = bank("ps_agg", 4)
        ps_t = bank("ps_t")
        ps_o = bank("ps_o")
        ps_l = bank("ps_l", 2)
        ps_h, ps_ht = ps_agg[:, 0:2, :], ps_agg[:, 2:4, :]

        x_in = [sem(f"x_in{g}") for g in range(NTG)]
        edges_in, small_in, w1_in, w2_in = sem("edges_in"), sem("small_in"), sem("w1_in"), sem("w2_in")
        parts_in, parts_out, parts_back = sem("parts_in"), sem("parts_out"), sem("parts_back")
        consts_ready, ones3_ready = sem("consts_ready"), sem("ones3_ready")
        dve_step, pool_step = sem("dve_step"), sem("pool_step")
        var_ready, std_ready = sem("var_ready"), sem("std_ready")
        xn_ready, xn_out = sem("xn_ready"), sem("xn_out")
        least_ready = sem("least_ready")
        edge_tables, bad_summed, bad_ready = sem("edge_tables"), sem("bad_summed"), sem("bad_ready")
        gathered = [sem(f"gathered{k}") for k in range(2 * CG)]
        staged = [sem(f"staged{k}") for k in range(2)]
        s_ready, group_done, group_added = sem("s_ready"), sem("group_done"), sem("group_added")
        r_gathered = [sem(f"r_gathered{k}") for k in range(CG)]
        r_staged, r_s, r_done, r_added, r_shift = (
            sem("r_staged"), sem("r_s"), sem("r_done"), sem("r_added"), sem("r_shift"))
        own_norm, own_tr, own_copied, agg_copied, nbr_done = (
            sem("own_norm"), sem("own_tr"), sem("own_copied"), sem("agg_copied"), sem("nbr_done"))
        half_sum, x1_ready, x1_out, stat1, var1, std1, rstd1 = (
            sem("half_sum"), sem("x1_ready"), sem("x1_out"), sem("stat1"), sem("var1"), sem("std1"), sem("rstd1"))
        z_ready, stat2, var2, std2, rstd2, zn_scale, zn_ready, zn_out = (
            sem("z_ready"), sem("stat2"), sem("var2"), sem("std2"), sem("rstd2"), sem("zn_scale"), sem("zn_ready"),
            sem("zn_out"))
        z_tr, z_copied, logit_done, logit_added = (
            sem("z_tr"), sem("z_copied"), sem("logit_done"), sem("logit_added"))
        carried, pool_carried = sem("carried"), sem("pool_carried")
        trash_zero, trash_out = sem("trash_zero"), sem("trash_out")
        shifted, exp_ready, masks_ready, ranks_ready = (
            sem("shifted"), sem("exp_ready"), sem("masks_ready"), sem("ranks_ready"))
        hot_ready, hot_used, slots_ready = sem("hot_ready"), sem("hot_used"), sem("slots_ready")
        m_staged, m_sstaged = sem("m_staged"), sem("m_sstaged")
        m_gath = [sem(f"m_gath{k}") for k in range(4)]
        m_tr, m_xt, m_h, m_gelu, m_ht, m_htc, m_y, m_yw = (
            sem("m_tr"), sem("m_xt"), sem("m_h"), sem("m_gelu"), sem("m_ht"), sem("m_htc"), sem("m_y"), sem("m_yw"))
        m_sum = sem("m_sum")

        x_v = x.rearrange("(g t p) d -> g p t d", g=NTG, p=P)
        xn_v = xn_dram.rearrange("(g t p) d -> g p t d", g=NTG, p=P)

        block = ctx.enter_context(nc.Block())

        @block.sync
        def _(sp):
            for g in range(NTG):
                sp.dma_start(xs[:, g * TG * D:(g + 1) * TG * D].rearrange("p (t d) -> p t d", t=TG),
                             x_v[g]).then_inc(x_in[g], 16)
            sp.dma_start(wnbr_sb.rearrange("p (k n) -> p k n", k=KD),
                         w_nbr.rearrange("(k p) n -> p k n", p=P)).then_inc(small_in, 16)
            sp.dma_start(wown_sb.rearrange("p (k n) -> p k n", k=KD),
                         w_own.rearrange("(k p) n -> p k n", p=P)).then_inc(small_in, 16)
            sp.dma_start(bias_sb[:, :], bias.rearrange("(a n) -> a n", a=1).to_broadcast([P, D])
                         ).then_inc(small_in, 16)
            sp.dma_start(br_sb[:, :], br.rearrange("(a n) -> a n", a=1).to_broadcast([P, E])
                         ).then_inc(small_in, 16)
            sp.dma_start(wr_sb[:, :], Wr).then_inc(small_in, 16)
            sp.dma_start(lng_sb[:, :], ln_g).then_inc(small_in, 16)
            sp.dma_start(lnb_sb[:, :], ln_b).then_inc(small_in, 16)
            sp.dma_start(bpart[:, 0:E * H // P], b1.rearrange("e (q n) -> (e q) n", q=P // E)).then_inc(parts_in, 16)
            sp.dma_start(b2part[:, 0:E * D // P], b2.rearrange("e (q n) -> (e q) n", q=P // E)).then_inc(parts_in, 16)
            for g in range(NTG):
                sp.wait_ge(xn_ready, g + 1)
                sp.dma_start(xn_v[g], xg_stage.rearrange("p (t d) -> p t d", t=TG)).then_inc(xn_out, 16)
            def stage(g, half):
                sp.dma_start(idx_stage[:, half * CG:(half + 1) * CG], src_t[:, ds(g * CG, CG)]
                             ).then_inc(staged[half], 16)

            stage(0, 0)
            stage(1, 1)
            for e in range(E):
                sp.dma_start(w1_sb[:, e * KD * H:(e + 1) * KD * H], W1[:, e, :]).then_inc(w1_in, 16)
            sp.wait_ge(trash_zero, 1)
            sp.dma_start(ex_dram[TRASH:TRASH + P, :], y[:, 0:D]).then_inc(trash_out, 16)
            sp.dma_start(out[TRASH:TRASH + P, :], y[:, 0:D]).then_inc(trash_out, 16)
            sp.wait_ge(parts_out, 6 * 16)
            sp.dma_start(b1s_sb[:, :], b1s_dram).then_inc(parts_back, 16)
            sp.dma_start(b2s_sb[:, :], b2s_dram).then_inc(parts_back, 16)

            def store(t):
                sp.wait_ge(x1_ready, t + 1)
                sp.dma_start(out[ds(t * P, P), :], xs[:, ds(t * D, D)]).then_inc(x1_out, 16)
                sp.wait_ge(zn_ready, t + 1)
                sp.dma_start(ex_dram[ds(t * P, P), :], zn[:, :]).then_inc(zn_out, 16)

            def iteration(i, chunks, tile):
                if chunks:
                    for half in range(2):
                        sp.wait_ge(group_done, 2 * i + half + 1)
                        stage(2 * i + 2 + half, half)
                if tile:
                    store(i - LAG - 1)

            with sp.Fori(0, LAG + 1) as i:
                iteration(i, True, False)
            with sp.Fori(LAG + 1, NIT - 1) as i:
                iteration(i, True, True)
            with sp.Fori(NIT - 1, NT + LAG + 1) as i:
                iteration(i, False, True)
            sp.wait_ge(x1_out, 16 * NT)
            sp.wait_ge(nbr_done, NT)
            for e in range(E):
                sp.dma_start(w2_sb[:, e * KH * D:(e + 1) * KH * D], W2[:, e, :]).then_inc(w2_in, 16)
            sp.wait_ge(trash_out, 32)

        @block.gpsimd
        def _(pool):
            n = 0
            for t, v in ((ident, 0.0), (lower, 1.0), (ones, 1.0), (eps_sb, EPS)):
                pool.memset(t[:, :], v).then_inc(pool_step, 1)
                n += 1
            pool.memset(y[:, 0:D], 0.0).then_inc(trash_zero, 1)
            pool.wait_ge(pool_step, n)
            pool.affine_select(out=ident[:, :], in_=ident[:, :], compare_op=ALU.not_equal, fill=1.0, base=0,
                               pattern=[[-1, P]], channel_multiplier=1).then_inc(consts_ready, 1)
            pool.affine_select(out=lower[:, :], in_=lower[:, :], compare_op=ALU.is_ge, fill=0.0, base=-1,
                               pattern=[[1, P]], channel_multiplier=-1).then_inc(consts_ready, 1)
            pool.iota(iota_f[:, :], [[1, P]], base=0, channel_multiplier=0,
                      allow_small_or_imprecise_dtypes=True).then_inc(consts_ready, 1)
            pool.iota(iota_e[:, :], [[0, NT], [1, E]], base=0, channel_multiplier=0,
                      allow_small_or_imprecise_dtypes=True).then_inc(consts_ready, 1)
            pool.iota(iota_e8[:, :], [[0, NT], [1, E]], base=E, channel_multiplier=0,
                      allow_small_or_imprecise_dtypes=True).then_inc(consts_ready, 1)
            pool.iota(node_id[:, :], [[P, NT]], base=1, channel_multiplier=1,
                      allow_small_or_imprecise_dtypes=True).then_inc(consts_ready, 1)
            pool.iota(trash_id[:, :], [[1, 1]], base=TRASH + 1, channel_multiplier=1,
                      allow_small_or_imprecise_dtypes=True).then_inc(consts_ready, 1)

            pool.iota(early_g[:, NG:2 * NG], [[P, NIT], [0, 2]], base=(1 - LAG) * P, channel_multiplier=0,
                      allow_small_or_imprecise_dtypes=True).then_inc(least_ready, 1)

            def gather(to, at, done):
                pool.indirect_dma_start(out=to, out_offset=None, in_=xn_dram,
                                        in_offset=bass.IndirectOffsetOnAxis(ap=at, axis=0)).then_inc(done, 16)

            pool.wait_ge(xn_out, 16 * NTG)
            pool.wait_ge(bad_ready, 1)
            bad = pool.value_load(bad_i[0:1, 0:1], min_val=0, max_val=1)
            with pool.If(bad):
                with pool.Fori(0, NT) as w:
                    with pool.Fori(0, NG) as g:
                        pool.wait_ge(r_done, w * NG + g + 1)
                        pool.dma_start(r_stage[:, :], src_t[:, ds(g * CG, CG)]).then_inc(r_staged, 16)
                        pool.wait_ge(r_staged, w * (16 * NG) + g * 16 + 16)
                        pool.sem_inc(pool_carried, 1)
                        for k in range(CG):
                            gather(G[:, k * D:(k + 1) * D], r_stage[:, k:k + 1], r_gathered[k])
                pool.wait_ge(r_done, NT * NG + 1)

            def fetch(i):
                for half in range(2):
                    pool.wait_ge(staged[half], 16 * i + 16)
                    pool.sem_inc(pool_carried, 1)
                    for k in range(CG):
                        c = half * CG + k
                        gather(G[:, c * D:(c + 1) * D], idx_stage[:, c:c + 1], gathered[c])

            with pool.Fori(0, NIT) as i:
                fetch(i)

            pool.wait_ge(slots_ready, 1)
            pool.wait_ge(zn_out, 16 * NT)
            pool.wait_ge(trash_out, 32)
            pool.wait_ge(x1_out, 16 * NT)

            def rows(a, k):
                if not (isinstance(a, int) and a < 4):
                    pool.wait_ge(m_tr, a - 3)
                pool.tensor_copy(gat_stage[:, k:k + 1], slot_idx[:, ds(a, 1)]).then_inc(m_staged, 1)
                pool.wait_ge(m_staged, a + 1)
                pool.sem_inc(pool_carried, 1)
                pool.indirect_dma_start(
                    out=xe[:, k * D:(k + 1) * D], out_offset=None, in_=ex_dram,
                    in_offset=bass.IndirectOffsetOnAxis(ap=gat_stage[:, k:k + 1], axis=0),
                ).then_inc(m_gath[k], 16)

            def add_rows(a, k):
                pool.tensor_copy(sca_stage[:, k:k + 1], slot_idx[:, ds(a, 1)]).then_inc(m_sstaged, 1)
                pool.wait_ge(m_sstaged, a + 1)
                pool.wait_ge(m_yw, a + 1)
                if not (isinstance(a, int) and a == 0):
                    pool.wait_ge(m_sum, 16 * a)
                pool.sem_inc(pool_carried, 1)
                pool.indirect_dma_start(
                    out=out, out_offset=bass.IndirectOffsetOnAxis(ap=sca_stage[:, k:k + 1], axis=0),
                    in_=y[:, k * D:(k + 1) * D], in_offset=None, compute_op=ALU.add,
                ).then_inc(m_sum, 16)

            for a in range(4):
                rows(a, a)
            for a in range(4):
                rows(a + 4, a)
                add_rows(a, a % 2)
            with pool.Fori(1, MT // 4 - 1) as i:
                for k in range(4):
                    rows(4 * i + (k + 4), k)
                    add_rows(4 * i + k, k % 2)
            for a in range(MT - 4, MT):
                add_rows(a, a % 2)
            pool.wait_ge(m_sum, 16 * MT)

        @block.vector
        def _(dve):
            steps = [0]

            def step(ins):
                steps[0] += 1
                ins.then_inc(dve_step, 1)
                dve.wait_ge(dve_step, steps[0])

            dve.memset(ones3[:, :], 1.0).then_inc(ones3_ready, 1)
            step(dve.memset(agg_t, 0.0))

            dve.wait_ge(edges_in, 48)
            step(dve.tensor_tensor(rel[:, :].rearrange("p (g k) -> p g k", k=CG),
                                   dst_sb[:, :].rearrange("p (g k) -> p g k", k=CG),
                                   first_sb[:, :].rearrange("p (g k) -> p g k", k=1).to_broadcast([P, NG, CG]),
                                   ALU.subtract))
            dve.tensor_scalar(inside[:, :], rel[:, :], 0.0, None, ALU.is_ge)
            step(dve.tensor_scalar(rest[:, :], rel[:, :], float(P), None, ALU.is_lt))
            step(dve.tensor_tensor(inside[:, :], inside[:, :], rest[:, :], ALU.mult))
            dve.tensor_copy(rest[:, :], dst_sb[:, :])
            dve.tensor_reduce(n_bad[:, 0:1], inside[:, :], AX.X, ALU.add)
            dve.wait_ge(consts_ready, 7)
            dve.wait_ge(least_ready, 1)
            step(dve.tensor_tensor(early_g[:, 0:NG], first_sb[:, :], early_g[:, NG:2 * NG], ALU.is_ge))
            step(dve.tensor_reduce(n_bad[:, 1:2], early_g[:, 0:NG], AX.X, ALU.add))
            step(dve.tensor_tensor(n_bad[:, 0:1], n_bad[:, 0:1], n_bad[:, 1:2], ALU.add))
            dve.tensor_scalar(n_bad[:, 2:3], n_bad[:, 0:1], -1.0, float(NCH + NG), ALU.mult, ALU.add
                              ).then_inc(edge_tables, 1)
            dve.wait_ge(bad_summed, 1)
            dve.tensor_scalar(good[:, :], ps_l[:, 0, 0:1], 0.0, None, ALU.is_equal)
            step(dve.tensor_scalar(bad_i[:, :], ps_l[:, 0, 0:1], 1.0, None, ALU.min))
            dve.sem_inc(bad_ready, 1)

            for g in range(NTG):
                dve.wait_ge(x_in[g], 16)
                for t in range(TG):
                    last = dve.bn_stats(stat[:, t * 6:t * 6 + 6], xs[:, (g * TG + t) * D:(g * TG + t + 1) * D])
                step(last)
                for t in range(TG):
                    last = dve.bn_aggr(mv[:, 2 * (g * TG + t):2 * (g * TG + t) + 2], stat[:, t * 6:t * 6 + 6])
                last.then_inc(var_ready, 1)
                dve.wait_ge(var_ready, g + 1)
                dve.wait_ge(std_ready, g + 1)
                step(dve.reciprocal(rstd[:, g * TG:(g + 1) * TG], rstd[:, g * TG:(g + 1) * TG]))
                if g:
                    dve.wait_ge(xn_out, 16 * g)
                for t in range(TG):
                    c = g * TG + t
                    last = dve.tensor_scalar(xg_stage[:, t * D:(t + 1) * D], xs[:, c * D:(c + 1) * D],
                                             mv[:, 2 * c:2 * c + 1], rstd[:, c:c + 1], ALU.subtract, ALU.mult)
                last.then_inc(xn_ready, 1)

            dve.wait_ge(parts_in, 32)
            for part, split, n in ((bpart, bsplit, E * H // P), (b2part, b2split, E * D // P)):
                a, b = part[:, 0:n], part[:, n:2 * n]
                step(dve.tensor_copy(split[:, 0:n], a))
                step(dve.tensor_tensor(b, a, split[:, 0:n], ALU.subtract))
                step(dve.tensor_copy(split[:, n:2 * n], b))
                step(dve.tensor_tensor(a, b, split[:, n:2 * n], ALU.subtract))
                dve.tensor_copy(split[:, 2 * n:3 * n], a).then_inc(parts_in, 1)

            dve.wait_ge(small_in, 7 * 16)

            def one_hots(table, c0, half, done):
                for k in range(CG):
                    s = half * CG + k
                    last = dve.tensor_scalar(S[:, s * P:(s + 1) * P], iota_f[:, :], table[:, ds(c0 + k, 1)],
                                             wgt_sb[:, ds(c0 + k, 1)], ALU.is_equal, ALU.mult)
                last.then_inc(done, 1)

            def sums(base, half, done):
                dve.tensor_tensor(agg_v[:, :, ds(base, P)], agg_v[:, :, ds(base, P)],
                                  ps_agg[:, 2 * half:2 * half + 2, 0:P], ALU.add).then_inc(done, 1)

            bad = dve.value_load(bad_i[0:1, 0:1], min_val=0, max_val=1)
            with dve.If(bad):
                dve.sem_inc(r_added, 1)
                dve.sem_inc(r_shift, 1)
                with dve.Fori(0, NT) as w:
                    with dve.Fori(0, NG) as g:
                        dve.wait_ge(r_done, w * NG + g + 1)
                        dve.wait_ge(r_shift, w + 1)
                        one_hots(rest, g * CG, 0, r_s)
                        dve.wait_ge(r_done, w * NG + g + 2)
                        dve.wait_ge(r_added, w * NG + g + 1)
                        sums(w * P, 0, r_added)
                    dve.tensor_scalar(rest[:, :], rest[:, :], float(-P), None, ALU.add).then_inc(r_shift, 1)
                dve.wait_ge(r_added, NT * NG + 1)
            dve.tensor_scalar(wgt_sb[:, :], wgt_sb[:, :], good[:, 0:1], None, ALU.mult)
            step(dve.tensor_scalar(first_sb[:, :], first_sb[:, :], float(-NROW), good[:, 0:1], ALU.add, ALU.mult))
            step(dve.tensor_scalar(first_sb[:, :], first_sb[:, :], float(NROW), None, ALU.add))

            def own_norm_of(t):
                if not (isinstance(t, int) and t == 0):
                    dve.wait_ge(own_tr, t)
                dve.tensor_scalar(one_tile[:, :], xs[:, ds(t * D, D)], mv[:, ds(2 * t, 1)], rstd[:, ds(t, 1)],
                                  ALU.subtract, ALU.mult).then_inc(own_norm, 1)

            def x1_of(t):
                at = xs[:, ds(t * D, D)]
                dve.wait_ge(nbr_done, t + 1)
                dve.tensor_tensor(at, at, ps_o[:, 0, 0:D], ALU.add).then_inc(half_sum, 1)
                dve.wait_ge(half_sum, t + 1)
                dve.tensor_tensor(at, at, bias_sb[:, :], ALU.add).then_inc(x1_ready, 1)
                dve.wait_ge(x1_ready, t + 1)
                dve.sem_inc(carried, 1)
                dve.bn_stats(stat[:, 0:6], at).then_inc(stat1, 1)
                dve.wait_ge(stat1, t + 1)
                dve.sem_inc(carried, 1)
                dve.bn_aggr(mv2[:, 0:2], stat[:, 0:6]).then_inc(var1, 1)

            def z_of(t):
                dve.wait_ge(std1, t + 1)
                dve.reciprocal(rs2[:, 0:1], rs2[:, 0:1]).then_inc(rstd1, 1)
                dve.wait_ge(rstd1, t + 1)
                if not (isinstance(t, int) and t == 0):
                    dve.wait_ge(z_tr, t)
                    dve.wait_ge(zn_ready, t)
                dve.tensor_scalar(zt[:, :], xs[:, ds(t * D, D)], mv2[:, 0:1], rs2[:, 0:1],
                                  ALU.subtract, ALU.mult).then_inc(z_ready, 1)
                dve.wait_ge(z_ready, t + 1)
                dve.sem_inc(carried, 1)
                dve.bn_stats(stat[:, 6:12], zt[:, :]).then_inc(stat2, 1)
                dve.wait_ge(stat2, t + 1)
                dve.sem_inc(carried, 1)
                dve.bn_aggr(mv2[:, 2:4], stat[:, 6:12]).then_inc(var2, 1)

            def zn_scale_of(t):
                dve.wait_ge(std2, t + 1)
                dve.reciprocal(rs2[:, 1:2], rs2[:, 1:2]).then_inc(rstd2, 1)
                dve.wait_ge(rstd2, t + 1)
                dve.scalar_tensor_tensor(out=nmr[:, :], in0=mv2[:, 2:3], scalar=-1.0, in1=rs2[:, 1:2],
                                         op0=ALU.mult, op1=ALU.mult).then_inc(zn_scale, 1)

            def logits_of(t):
                dve.wait_ge(logit_done, t + 1)
                dve.tensor_tensor(logit[:, ds(t * E, E)], ps_l[:, 1, 0:E], br_sb[:, :], ALU.add
                                  ).then_inc(logit_added, 1)

            def iteration(i, chunks, norm, tile):
                if norm:
                    own_norm_of(i - LAG)
                if tile:
                    x1_of(i - LAG - 1)
                if chunks:
                    if not (isinstance(i, int) and i == 0):
                        dve.wait_ge(group_done, 2 * i - 1)
                    one_hots(rel, i * (2 * CG), 0, s_ready)
                if tile:
                    z_of(i - LAG - 1)
                if chunks:
                    if not (isinstance(i, int) and i == 0):
                        dve.wait_ge(group_done, 2 * i)
                    one_hots(rel, i * (2 * CG) + CG, 1, s_ready)
                if tile:
                    zn_scale_of(i - LAG - 1)
                if chunks:
                    for half in range(2):
                        g = 2 * i + half
                        base = dve.value_load(first_sb[0:1, ds(g, 1)], min_val=0, max_val=NROW)
                        dve.wait_ge(group_done, g + 1)
                        if not (isinstance(g, int) and g == 0):
                            dve.wait_ge(group_added, g)
                        sums(base, half, group_added)
                if tile:
                    logits_of(i - LAG - 1)

            iteration(0, True, False, False)
            with dve.Fori(1, LAG) as i:
                iteration(i, True, False, False)
            iteration(LAG, True, True, False)
            iteration(LAG + 1, True, True, True)
            with dve.Fori(LAG + 2, NIT) as i:
                iteration(i, True, True, True)
            with dve.Fori(NIT, NT + LAG) as i:
                iteration(i, False, True, True)
            iteration(NT + LAG, False, False, True)

            def te(t):
                return t[:, :].rearrange("p (t e) -> p t e", e=E)

            def over_e(v):
                return v[:, :].rearrange("p (t a) -> p t a", a=1).to_broadcast([P, NT, E])

            pr, m1, m2, a, b, c, sl = small
            mx, sm, p1, i1, p2, i2, valid, tokv, w1v, w2v = per
            dve.wait_ge(logit_added, NT)
            step(dve.tensor_reduce(mx[:, :], te(logit), AX.X, ALU.max))
            dve.tensor_tensor(te(a), te(logit), over_e(mx), ALU.subtract).then_inc(shifted, 1)
            dve.tensor_scalar(valid[:, :], node_id[:, :], float(N), None, ALU.is_le)
            dve.wait_ge(exp_ready, 1)
            step(dve.tensor_reduce(sm[:, :], te(b), AX.X, ALU.add))
            step(dve.reciprocal(sm[:, :], sm[:, :]))
            step(dve.tensor_tensor(te(pr), te(b), over_e(sm), ALU.mult))
            for mask, best, at in ((m1, p1, i1), (m2, p2, i2)):
                step(dve.tensor_reduce(best[:, :], te(pr), AX.X, ALU.max))
                step(dve.tensor_tensor(te(a), te(pr), over_e(best), ALU.is_equal))
                step(dve.scalar_tensor_tensor(out=b[:, :], in0=a[:, :], scalar=float(-E), in1=iota_e8[:, :],
                                              op0=ALU.mult, op1=ALU.add))
                step(dve.tensor_reduce(at[:, :], te(b), AX.X, ALU.min))
                step(dve.tensor_tensor(te(mask), te(iota_e), over_e(at), ALU.is_equal))
                if mask is m1:
                    step(dve.scalar_tensor_tensor(out=pr[:, :], in0=mask[:, :], scalar=-2.0, in1=pr[:, :],
                                                  op0=ALU.mult, op1=ALU.add))
            step(dve.tensor_tensor(te(m1), te(m1), over_e(valid), ALU.mult))
            step(dve.tensor_tensor(te(m2), te(m2), over_e(valid), ALU.mult))
            dve.tensor_tensor(a[:, :].rearrange("p (e t) -> p t e", e=E), te(m1), te(m2), ALU.add
                              ).then_inc(masks_ready, 1)
            step(dve.tensor_tensor(sm[:, :], p1[:, :], p2[:, :], ALU.add))
            step(dve.reciprocal(sm[:, :], sm[:, :]))
            step(dve.tensor_tensor(sm[:, :], sm[:, :], valid[:, :], ALU.mult))
            dve.tensor_tensor(w1v[:, :], p1[:, :], sm[:, :], ALU.mult)
            dve.tensor_tensor(w2v[:, :], p2[:, :], sm[:, :], ALU.mult)
            step(dve.tensor_tensor(tokv[:, :], node_id[:, :], valid[:, :], ALU.mult))

            dve.wait_ge(ranks_ready, 1)
            step(dve.tensor_copy(b[:, :], ps_l[:, 1, 0:NT * E]))
            step(dve.memset(c[:, :], 1.0))
            step(dve.tensor_tensor_scan(sl[:, :], c[:, :], b[:, :], 0.0, ALU.mult, ALU.add))
            cnt, start, tiles, upto, tbase, off = per_e
            sl_e = sl[:, :].rearrange("p (e t) -> p e t", e=E)
            step(dve.tensor_tensor(b[:, :], sl[:, :], b[:, :], ALU.subtract))
            b_e = b[:, :].rearrange("p (e t) -> p e t", e=E)
            step(dve.tensor_copy(start[:, :], b_e[:, :, 0]))
            step(dve.tensor_tensor(cnt[:, :], sl_e[:, :, NT - 1], start[:, :], ALU.subtract))
            step(dve.tensor_scalar(cnt_i[:, 0:E], cnt[:, :], float(P - 1), None, ALU.add))
            step(dve.tensor_scalar(cnt_i[:, E:2 * E], cnt_i[:, 0:E], 7, None, ALU.arith_shift_right))
            step(dve.tensor_copy(tiles[:, :], cnt_i[:, E:2 * E]))
            step(dve.tensor_tensor_scan(upto[:, :], c[:, 0:E], tiles[:, :], 0.0, ALU.mult, ALU.add))
            step(dve.tensor_tensor(tbase[:, :], upto[:, :], tiles[:, :], ALU.subtract))
            step(dve.scalar_tensor_tensor(out=off[:, :], in0=tbase[:, :], scalar=float(P), in1=start[:, :],
                                          op0=ALU.mult, op1=ALU.subtract))
            step(dve.tensor_tensor(b[:, :], b[:, :], ps_l[:, 0, 0:NT * E], ALU.add))
            step(dve.tensor_tensor(te(sl), b[:, :].rearrange("p (e t) -> p t e", e=E),
                                   off[:, :].rearrange("p (a e) -> p a e", a=1).to_broadcast([P, NT, E]), ALU.add))
            for k, mask in enumerate((m1, m2)):
                step(dve.tensor_tensor(te(a), te(mask), te(sl), ALU.mult))
                step(dve.tensor_reduce(mx[:, :], te(a), AX.X, ALU.add))
                step(dve.tensor_copy(slot_i[:, k * NT:(k + 1) * NT], mx[:, :]))
                at = slot_i[:, k * NT:(k + 1) * NT]
                dve.tensor_scalar(part_i[:, 2 * k * NT:(2 * k + 1) * NT], at, 7, None, ALU.arith_shift_right)
                step(dve.tensor_scalar(part_i[:, (2 * k + 1) * NT:(2 * k + 2) * NT], at, P - 1, None, ALU.bitwise_and))
            step(dve.tensor_copy(place[:, :], part_i[:, :]))

            step(dve.tensor_scalar(tile_e[:, :], iota_f[:, 0:MT], tbase[:, 1:2], None, ALU.is_ge))
            for e in range(2, E):
                step(dve.scalar_tensor_tensor(out=tile_e[:, :], in0=iota_f[:, 0:MT], scalar=tbase[:, e:e + 1],
                                              in1=tile_e[:, :], op0=ALU.is_ge, op1=ALU.add))
            step(dve.tensor_copy(tile_ei[:, :], tile_e[:, :]))

            def slots_of(t, first):
                for k, wv in enumerate((w1v, w2v)):
                    if not first:
                        dve.wait_ge(hot_used, 2 * t + k - 1)
                    o = k * 2 * MT
                    dve.tensor_scalar(hot_row[:, k * P:(k + 1) * P], iota_f[:, :],
                                      place[:, ds((2 * k + 1) * NT + t, 1)], None, ALU.is_equal)
                    dve.tensor_scalar(hot_tile[:, o:o + MT], iota_f[:, 0:MT], place[:, ds(2 * k * NT + t, 1)],
                                      tokv[:, ds(t, 1)], ALU.is_equal, ALU.mult)
                    dve.tensor_scalar(hot_tile[:, o + MT:o + 2 * MT], iota_f[:, 0:MT],
                                      place[:, ds(2 * k * NT + t, 1)], wv[:, ds(t, 1)], ALU.is_equal, ALU.mult
                                      ).then_inc(hot_ready, 1)

            slots_of(0, True)
            with dve.Fori(1, NT) as t:
                slots_of(t, False)
            dve.wait_ge(hot_used, 2 * NT)
            step(dve.tensor_copy(tok[:, :], ps_o[:, 0, 0:2 * MT]))
            step(dve.tensor_scalar(tile_e[:, :], tok[:, 0:MT], 0.0, trash_id[:, :], ALU.is_equal, ALU.mult))
            step(dve.scalar_tensor_tensor(out=tile_e[:, :], in0=tile_e[:, :], scalar=-1.0, in1=tok[:, 0:MT],
                                          op0=ALU.add, op1=ALU.add))
            dve.tensor_copy(slot_idx[:, :], tile_e[:, :]).then_inc(slots_ready, 1)

            def hidden_copy(a):
                for n in range(2):
                    dve.wait_ge(m_ht, 2 * a + n + 1)
                    if n == 0 and not (isinstance(a, int) and a == 0):
                        dve.wait_ge(m_y, a)
                    dve.tensor_copy(hid_t[:, n * 512:(n + 1) * 512], ps_ht[:, n, :]).then_inc(m_htc, 1)

            def weigh(a, k):
                dve.wait_ge(m_y, a + 1)
                if not (isinstance(a, int) and a < 2):
                    dve.wait_ge(m_sum, 16 * a - 16)
                dve.tensor_scalar(y[:, k * D:(k + 1) * D], ps_o[:, 0, 0:D], tok[:, ds(a + MT, 1)], None, ALU.mult
                                  ).then_inc(m_yw, 1)

            dve.wait_ge(trash_out, 32)
            hidden_copy(0)
            weigh(0, 0)
            hidden_copy(1)
            weigh(1, 1)
            with dve.Fori(1, MT // 2) as i:
                for k in range(2):
                    hidden_copy(2 * i + k)
                    weigh(2 * i + k, k)

        @block.scalar
        def _(act):
            act.dma_start(dst_sb[:, :], dst_t).then_inc(edges_in, 16)
            act.dma_start(wgt_sb[:, :], wgt_t).then_inc(edges_in, 16)
            act.dma_start(first_sb[:, :], dst_first.to_broadcast([P, NG])).then_inc(edges_in, 16)
            act.wait_ge(consts_ready, 1)
            for g in range(NTG):
                act.wait_ge(var_ready, g + 1)
                v = mv[:, 2 * g * TG:2 * (g + 1) * TG]
                act.activation(rstd[:, g * TG:(g + 1) * TG], v[:, 1:2 * TG:2], ACT.Sqrt, bias=eps_sb[:, :]
                               ).then_inc(std_ready, 1)
            act.wait_ge(parts_in, 34)
            for split, dram, n in ((bsplit, b1s_dram, E * H // P), (b2split, b2s_dram, E * D // P)):
                for j in range(3):
                    act.dma_start(dram[j:j + 1, :].rearrange("a (p n) -> (a p) n", p=P),
                                  split[:, j * n:(j + 1) * n]).then_inc(parts_out, 16)

            def copies(t):
                if not (isinstance(t, int) and t == 0):
                    act.wait_ge(nbr_done, t)
                act.wait_ge(group_added, 2 * t + 2 * LAG)
                act.activation(tile_t[:, 0:KD * P].rearrange("p (k n) -> p k n", k=KD),
                               agg_v[:, :, ds(t * P, P)], ACT.Copy).then_inc(agg_copied, 1)
                act.wait_ge(own_tr, t + 1)
                act.activation(tile_t[:, KD * P:2 * KD * P], ps_t[:, 0, 0:KD * P], ACT.Copy).then_inc(own_copied, 1)

            def iteration(i, norm, tile):
                t = i - LAG - 1
                if tile:
                    act.wait_ge(var1, t + 1)
                    act.activation(rs2[:, 0:1], mv2[:, 1:2], ACT.Sqrt, bias=eps_sb[:, :]).then_inc(std1, 1)
                if norm:
                    copies(i - LAG)
                if tile:
                    act.wait_ge(var2, t + 1)
                    act.activation(rs2[:, 1:2], mv2[:, 3:4], ACT.Sqrt, bias=eps_sb[:, :]).then_inc(std2, 1)
                    act.wait_ge(zn_scale, t + 1)
                    if not (isinstance(t, int) and t == 0):
                        act.wait_ge(zn_out, 16 * t)
                    act.activation(zn[:, :], zt[:, :], ACT.Identity, bias=nmr[:, 0:1], scale=rs2[:, 1:2]
                                   ).then_inc(zn_ready, 1)
                    act.wait_ge(z_tr, t + 1)
                    if not (isinstance(t, int) and t == 0):
                        act.wait_ge(logit_done, t)
                    act.activation(z_t[:, :], ps_l[:, 0, 0:KD * P], ACT.Copy).then_inc(z_copied, 1)

            iteration(LAG, True, False)
            iteration(LAG + 1, True, True)
            with act.Fori(LAG + 2, NIT) as i:
                iteration(i, True, True)

            def last_copies(t):
                act.wait_ge(nbr_done, t)
                act.wait_ge(group_added, NG)
                act.activation(tile_t[:, 0:KD * P].rearrange("p (k n) -> p k n", k=KD),
                               agg_v[:, :, ds(t * P, P)], ACT.Copy).then_inc(agg_copied, 1)
                act.wait_ge(own_tr, t + 1)
                act.activation(tile_t[:, KD * P:2 * KD * P], ps_t[:, 0, 0:KD * P], ACT.Copy).then_inc(own_copied, 1)

            copies = last_copies
            with act.Fori(NIT, NT + LAG) as i:
                iteration(i, True, True)
            iteration(NT + LAG, False, True)

            act.wait_ge(shifted, 1)
            act.activation(small[4][:, :], small[3][:, :], ACT.Exp).then_inc(exp_ready, 1)

            act.wait_ge(slots_ready, 1)

            def scaled(a, k):
                e = act.value_load(tile_ei[0:1, ds(a, 1)], min_val=0, max_val=E - 1)
                act.wait_ge(m_tr, a + 1)
                if not (isinstance(a, int) and a < 2):
                    act.wait_ge(m_h, 2 * a - 2)
                for d in range(KD):
                    last = act.activation(xe_t[:, (k * KD + d) * P:(k * KD + d + 1) * P],
                                          ps_t[:, 0, d * P:(d + 1) * P], ACT.Identity,
                                          bias=lnb_sb[:, ds(e + d * E, 1)], scale=lng_sb[:, ds(e + d * E, 1)])
                last.then_inc(m_xt, 1)

            def gelu(a):
                for n in range(2):
                    act.wait_ge(m_h, 2 * a + n + 1)
                    if n == 0 and not (isinstance(a, int) and a == 0):
                        act.wait_ge(m_ht, 2 * a)
                    act.activation(hid[:, n * 512:(n + 1) * 512], ps_h[:, n, :], ACT.Gelu).then_inc(m_gelu, 1)

            scaled(0, 0)
            scaled(1, 1)
            gelu(0)
            with act.Fori(1, MT // 2) as i:
                scaled(2 * i, 0)
                gelu(2 * i - 1)
                scaled(2 * i + 1, 1)
                gelu(2 * i)
            gelu(MT - 1)

        @block.tensor
        def _(pe):
            pe.wait_ge(edge_tables, 1)
            pe.wait_ge(consts_ready, 7)
            pe.matmul(ps_l[:, 0, 0:1], ones[:, :], n_bad[:, 2:3], start=True, stop=True).then_inc(bad_summed, 1)
            pe.wait_ge(small_in, 7 * 16)

            def products(half, rows_in, count, ready, count_s, free, count_f, done):
                for k in range(CG):
                    s = half * CG + k
                    pe.wait_ge(rows_in[s], count)
                    if k == 0:
                        pe.wait_ge(ready, count_s)
                        if count_f is not None:
                            pe.wait_ge(free, count_f)
                    for d in range(KD):
                        last = pe.matmul(ps_agg[:, 2 * half + d, 0:P], G[:, s * D + d * P:s * D + (d + 1) * P],
                                         S[:, s * P:(s + 1) * P], start=(k == 0), stop=(k == CG - 1))
                last.then_inc(done, 1)

            pe.wait_ge(bad_ready, 1)
            bad = pe.value_load(bad_i[0:1, 0:1], min_val=0, max_val=1)
            with pe.If(bad):
                pe.sem_inc(r_done, 1)
                with pe.Fori(0, NT) as w:
                    with pe.Fori(0, NG) as g:
                        products(0, r_gathered, w * (16 * NG) + g * 16 + 16, r_s, w * NG + g + 1,
                                 r_added, w * NG + g + 1, r_done)
                pe.wait_ge(r_added, NT * NG + 1)

            def group(i, half):
                first = isinstance(i, int) and i == 0
                products(half, gathered, 16 * i + 16, s_ready, 2 * i + half + 1,
                         group_added, None if first else 2 * i + half - 1, group_done)

            def own_transpose(t):
                pe.wait_ge(own_norm, t + 1)
                if not (isinstance(t, int) and t == 0):
                    pe.wait_ge(own_copied, t)
                for d in range(KD):
                    last = pe.transpose(ps_t[:, 0, d * P:(d + 1) * P], one_tile[:, d * P:(d + 1) * P], ident[:, :])
                last.then_inc(own_tr, 1)

            def node_product(t):
                pe.wait_ge(agg_copied, t + 1)
                pe.wait_ge(own_copied, t + 1)
                if not (isinstance(t, int) and t == 0):
                    pe.wait_ge(half_sum, t)
                for j, w in ((0, wnbr_sb), (1, wown_sb)):
                    for d in range(KD):
                        last = pe.matmul(ps_o[:, 0, 0:D], tile_t[:, (j * KD + d) * P:(j * KD + d + 1) * P],
                                         w[:, d * D:(d + 1) * D], start=(j + d == 0), stop=(j + d == KD))
                last.then_inc(nbr_done, 1)

            def z_transpose(t):
                pe.wait_ge(z_ready, t + 1)
                if not (isinstance(t, int) and t == 0):
                    pe.wait_ge(z_copied, t)
                for d in range(KD):
                    last = pe.transpose(ps_l[:, 0, d * P:(d + 1) * P], zt[:, d * P:(d + 1) * P], ident[:, :])
                last.then_inc(z_tr, 1)

            def logits_of(t):
                pe.wait_ge(z_copied, t + 1)
                if not (isinstance(t, int) and t == 0):
                    pe.wait_ge(logit_added, t)
                for d in range(KD):
                    last = pe.matmul(ps_l[:, 1, 0:E], z_t[:, d * P:(d + 1) * P], wr_sb[:, d * E:(d + 1) * E],
                                     start=(d == 0), stop=(d == KD - 1))
                last.then_inc(logit_done, 1)

            def iteration(i, chunks, norm, tile):
                if norm:
                    own_transpose(i - LAG)
                if chunks:
                    group(i, 0)
                if norm:
                    node_product(i - LAG)
                if tile:
                    z_transpose(i - LAG - 1)
                if chunks:
                    group(i, 1)
                if tile:
                    logits_of(i - LAG - 1)

            iteration(0, True, False, False)
            with pe.Fori(1, LAG) as i:
                iteration(i, True, False, False)
            iteration(LAG, True, True, False)
            iteration(LAG + 1, True, True, True)
            with pe.Fori(LAG + 2, NIT) as i:
                iteration(i, True, True, True)
            with pe.Fori(NIT, NT + LAG) as i:
                iteration(i, False, True, True)
            iteration(NT + LAG, False, False, True)

            pe.wait_ge(masks_ready, 1)
            pe.matmul(ps_l[:, 0, 0:NT * E], lower[:, :], small[3][:, :], start=True, stop=True)
            pe.matmul(ps_l[:, 1, 0:NT * E], ones[:, :], small[3][:, :], start=True, stop=True).then_inc(ranks_ready, 1)

            def slots_of(t, first, final):
                for k in range(2):
                    pe.wait_ge(hot_ready, 2 * t + k + 1)
                    pe.matmul(ps_o[:, 0, 0:2 * MT], hot_row[:, k * P:(k + 1) * P],
                              hot_tile[:, k * 2 * MT:(k + 1) * 2 * MT], start=(first and k == 0),
                              stop=(final and k == 1), skip_group_check=True).then_inc(hot_used, 1)

            pe.wait_ge(half_sum, NT)
            slots_of(0, True, False)
            with pe.Fori(1, NT - 1) as t:
                slots_of(t, False, False)
            slots_of(NT - 1, False, True)

            pe.wait_ge(slots_ready, 1)
            pe.wait_ge(w1_in, 16 * E)
            pe.wait_ge(w2_in, 16 * E)
            pe.wait_ge(parts_back, 32)
            pe.wait_ge(ones3_ready, 1)

            def expert(a):
                return pe.value_load(tile_ei[0:1, ds(a, 1)], min_val=0, max_val=E - 1)

            def rows_t(a, k, n):
                pe.wait_ge(m_gath[k], n)
                if not (isinstance(a, int) and a == 0):
                    pe.wait_ge(m_xt, a)
                for d in range(KD):
                    last = pe.transpose(ps_t[:, 0, d * P:(d + 1) * P], xe[:, k * D + d * P:k * D + (d + 1) * P],
                                        ident[:, :])
                last.then_inc(m_tr, 1)

            def layer1(a, k, e):
                pe.wait_ge(m_xt, a + 1)
                for n in range(2):
                    if not (isinstance(a, int) and a == 0):
                        pe.wait_ge(m_gelu, 2 * a - 1 + n)
                    pe.matmul(ps_h[:, n, :], ones3[:, :], b1s_sb[:, ds(e * H + n * 512, 512)], start=True, stop=False)
                    for d in range(KD):
                        last = pe.matmul(ps_h[:, n, :], xe_t[:, (k * KD + d) * P:(k * KD + d + 1) * P],
                                         w1_sb[:, ds(e * (KD * H) + d * H + n * 512, 512)],
                                         start=False, stop=(d == KD - 1))
                    last.then_inc(m_h, 1)

            def layer2(a, e):
                if not (isinstance(a, int) and a == 0):
                    pe.wait_ge(m_yw, a)
                pe.matmul(ps_o[:, 0, 0:D], ones3[:, :], b2s_sb[:, ds(e * D, D)], start=True, stop=False)
                for j in range(KH):
                    if j % 4 == 0:
                        pe.wait_ge(m_htc, 2 * a + j // 4 + 1)
                    last = pe.matmul(ps_o[:, 0, 0:D], hid_t[:, j * P:(j + 1) * P],
                                     w2_sb[:, ds(e * (KH * D) + j * D, D)], start=False, stop=(j == KH - 1))
                last.then_inc(m_y, 1)

            def hidden_t(a):
                for n in range(2):
                    pe.wait_ge(m_gelu, 2 * a + n + 1)
                    if not (isinstance(a, int) and a == 0):
                        pe.wait_ge(m_htc, 2 * a - 1 + n)
                    for j in range(4):
                        last = pe.transpose(ps_ht[:, n, j * P:(j + 1) * P],
                                            hid[:, (4 * n + j) * P:(4 * n + j + 1) * P], ident[:, :])
                    last.then_inc(m_ht, 1)

            rows_t(0, 0, 16)

            def tile(a, k, rows_ahead):
                if rows_ahead is not None:
                    rows_t(a + 1, (k + 1) % 4, rows_ahead)
                layer1(a, k % 2, expert(a))
                if not (isinstance(a, int) and a == 0):
                    layer2(a - 1, expert(a - 1))
                hidden_t(a)

            for a in range(4):
                tile(a, a, 32 if a == 3 else 16)
            with pe.Fori(1, MT // 4 - 1) as i:
                for k in range(4):
                    tile(4 * i + k, k, 16 * i + (32 if k == 3 else 16))
            for k in range(4):
                tile(MT - 4 + k, k, None if k == 3 else 4 * MT)
            layer2(MT - 1, expert(MT - 1))


def kernel(x, src, dst, edge_weight, L0_gnn_w_nbr, L0_gnn_w_own, L0_gnn_bias, L0_ffn_Wr, L0_ffn_br, L0_ffn_ln_g,
           L0_ffn_ln_b, L0_ffn_W1, L0_ffn_b1, L0_ffn_W2, L0_ffn_b2):
    import numpy as np
    import concourse.bacc as bacc
    from concourse.bass_utils import run_bass_kernel_spmd

    n, d = x.shape
    rows = -(-n // P) * P
    per_it = 2 * CHUNKS_PER_GROUP * P
    edges = -(-len(src) // per_it) * per_it
    experts, _, hidden = L0_ffn_W1.shape

    def chunks(v, mode="constant"):
        return np.pad(np.asarray(v), (0, edges - len(v)), mode=mode).reshape(-1, P)

    dst_c = chunks(dst, "edge")
    arrays = {
        "x": np.pad(np.asarray(x), ((0, rows - n), (0, 0))),
        "src_t": np.ascontiguousarray(chunks(src).T),
        "dst_t": np.ascontiguousarray(dst_c.T),
        "dst_first": np.ascontiguousarray(dst_c[::CHUNKS_PER_GROUP, 0].reshape(1, -1)),
        "wgt_t": np.ascontiguousarray(chunks(edge_weight).T),
        "w_nbr": np.asarray(L0_gnn_w_nbr), "w_own": np.asarray(L0_gnn_w_own), "bias": np.asarray(L0_gnn_bias),
        "Wr": np.ascontiguousarray(np.asarray(L0_ffn_Wr).reshape(-1, P, experts).transpose(1, 0, 2).reshape(P, -1)),
        "br": np.asarray(L0_ffn_br),
        "ln_g": np.ascontiguousarray(np.asarray(L0_ffn_ln_g).reshape(experts, -1, P).transpose(2, 1, 0).reshape(P, -1)),
        "ln_b": np.ascontiguousarray(np.asarray(L0_ffn_ln_b).reshape(experts, -1, P).transpose(2, 1, 0).reshape(P, -1)),
        "W1": np.ascontiguousarray(np.asarray(L0_ffn_W1).reshape(experts, -1, P, hidden).transpose(2, 0, 1, 3)
                                   .reshape(P, experts, -1)),
        "b1": np.asarray(L0_ffn_b1),
        "W2": np.ascontiguousarray(np.asarray(L0_ffn_W2).reshape(experts, -1, P, d).transpose(2, 0, 1, 3)
                                   .reshape(P, experts, -1)),
        "b2": np.asarray(L0_ffn_b2),
    }
    nc = bacc.Bacc("TRN2", target_bir_lowering=False, num_devices=1)
    args = [nc.dram_tensor(k, v.shape, mybir.dt.from_np(v.dtype), kind="ExternalInput").ap()
            for k, v in arrays.items()]
    out = nc.dram_tensor("out", (rows + P, d), F32, kind="ExternalOutput").ap()
    gnn_moe(nc, *args, out)
    r = run_bass_kernel_spmd(nc, [arrays], core_ids=[0])
    return r.results[0]["out"][:n]
```

```python
from contextlib import ExitStack

import concourse.bass as bass
from concourse import mybir

P = 128
F32 = mybir.dt.float32
I32 = mybir.dt.int32
ALU = mybir.AluOpType
ACT = mybir.ActivationFunctionType
AX = mybir.AxisListType
ds = bass.ds

CHUNKS_PER_GROUP = 7
LAG = 5
EPS = 1e-5


def gnn_moe(nc, x, src_t, dst_t, dst_first, wgt_t, w_nbr, w_own, bias, Wr, br, ln_g, ln_b, W1, b1, W2, b2, out):
    D = x.shape[1]
    NT = x.shape[0] // P
    N = 3125
    NROW = NT * P
    NCH = src_t.shape[1]
    CG = CHUNKS_PER_GROUP
    NG = NCH // CG
    NIT = NG // 2
    E = b1.shape[0]
    H = b1.shape[1]
    KD, KH = D // P, H // P
    MT = (2 * N + E * (P - 1)) // P
    SURE = 2 * N // P // 4 * 4
    TG = 5
    NTG = NT // TG
    BY_ACT = 4
    FIRST = NIT - 1 - LAG
    SOON = 2
    AW = NROW + P
    TRASH = NROW
    assert NCH == 2 * NIT * CG and NT == TG * NTG and KD == 2 and MT % 4 == 0
    assert SOON * KH <= NIT - LAG and NIT == NT - 2 + LAG and SOON * H <= 2 * TG * D
    assert LAG + 2 < NT < NIT - 1 and NIT < NT + LAG and LAG + E * KD < NIT - 1

    ctx = ExitStack()
    with ctx:
        def sb(name, cols, dt=F32, parts=P):
            return ctx.enter_context(nc.sbuf_tensor(name, [parts, cols], dt))

        def bank(name, n=1):
            return ctx.enter_context(nc.psum_tensor(name, [P, n, 512], F32))

        def sem(name):
            return ctx.enter_context(nc.semaphore(name))

        xn_dram = nc.dram_tensor("xn_dram", [NROW, D], F32).ap()
        ex_dram = nc.dram_tensor("ex_dram", [NROW + P, D], F32).ap()

        w1_sb = sb("w1_sb", E * KD * H)
        w2_sb = sb("w2_sb", E * KH * D)
        cut = [0]

        def early(cols):
            cut[0] += cols
            assert cut[0] <= E * KH * D
            return w2_sb[:, cut[0] - cols:cut[0]]

        xs = early(NT * D)
        agg_t = early(KD * AW)
        agg_v = agg_t.rearrange("p (k n) -> p k n", k=KD)
        wnbr_sb, wown_sb = early(KD * D), early(KD * D)
        b2_sb = sb("b2_sb", E * D)
        b1_sb = sb("b1_sb", E * H)
        cut_b = [0]

        def early_b(cols):
            cut_b[0] += cols
            assert cut_b[0] <= E * H
            return b1_sb[:, cut_b[0] - cols:cut_b[0]]

        xg_stage = [early_b(TG * D), early_b(TG * D), early(TG * D)]
        NXG = len(xg_stage)
        S = early_b(2 * CG * P)
        wgt_sb = early_b(NCH)
        rel = early_b(NCH)
        rest = early_b(NCH)
        inside = early_b(NCH)
        one_tile = early_b(D)
        own_t = early_b(KD * P)
        agg_in, zt, zn, z_t = [[early_b(D), xg_stage[2][:, k * D:(k + 1) * D]] for k in range(4)]
        G = sb("G", 2 * CG * D)
        dst_sb = sb("dst_sb", NCH, I32)
        first_sb = sb("first_sb", NG, I32)
        early_g = sb("early_g", 2 * NG)
        idx_stage, r_stage = sb("idx_stage", 2 * CG, I32), sb("r_stage", CG, I32)
        n_bad = sb("n_bad", 3)
        good = sb("good", 1)
        bad_i = sb("bad_i", 1, I32)
        ident, iota_f, ones, lower = sb("ident", P), sb("iota_f", P), sb("ones", P), sb("lower", P)
        iota_e, iota_e8 = sb("iota_e", NT * E), sb("iota_e8", NT * E)
        node_id = sb("node_id", NT)
        trash_id = sb("trash_id", 1)
        eps_sb = sb("eps_sb", 1)
        bias_sb = sb("bias_sb", D)
        br_sb = sb("br_sb", E)
        wr_sb = sb("wr_sb", KD * E)
        lng_sb, lnb_sb = sb("lng_sb", KD * E), sb("lnb_sb", KD * E)
        stat = sb("stat", 2 * TG * 6)
        mv = sb("mv", NT * 2)
        rstd, nmr_x = sb("rstd", NT), sb("nmr_x", NT)
        mv2, rs2 = [sb(f"mv2_{k}", 4) for k in range(2)], [sb(f"rs2_{k}", 2) for k in range(2)]
        nmr = [sb(f"nmr{k}", 1) for k in range(2)]
        logit = sb("logit", NT * E)
        ones_te = sb("ones_te", NT * E)
        both_masks = sb("both_masks", 2 * NT * E)
        probs, is_best, work, logit_less, expo, chosen, slots = [
            sb(name, NT * E)[:, :] for name in ("probs", "is_best", "work", "logit_less", "expo", "chosen", "slots")]
        mx, sm, p1, i1, p2, i2, valid, tokv, w1v, w2v = [
            sb(name, NT) for name in ("mx", "sm", "p1", "i1", "p2", "i2", "valid", "tokv", "w1v", "w2v")]
        slot_f, slot_i = sb("slot_f", 2 * NT), sb("slot_i", 2 * NT, I32)
        part_i = sb("part_i", 4 * NT, I32)
        place = sb("place", 4 * NT)
        cnt, tiles, upto, tbase, off = [sb(name, E) for name in ("cnt", "tiles", "upto", "tbase", "off")]
        cnt_i = sb("cnt_i", 2 * E, I32)
        hot_row, hot_tile, hot_one = (
            G[:, 0:2 * TG * P], G[:, 2 * TG * P:2 * TG * P + 4 * TG * MT],
            G[:, 2 * TG * P + 4 * TG * MT:2 * TG * P + 6 * TG * MT])
        tok = sb("tok", 2 * MT)
        slot_idx = sb("slot_idx", MT, I32)
        tile_e, tile_ei = sb("tile_e", MT), sb("tile_ei", MT, I32)
        tile_of, tile_after = sb("tile_of", MT), sb("tile_after", 2 * MT)
        tile_used, last_tile = sb("tile_used", MT, I32), sb("last_tile", 1, I32)
        gat_stage, sca_stage = sb("gat_stage", 4, I32), sb("sca_stage", 2, I32)
        hid, hid_t, xe, xe_t = G[:, 0:H], G[:, H:2 * H], G[:, 2 * H:2 * H + 4 * D], G[:, 2 * H + 4 * D:2 * H + 6 * D]
        y = sb("y", 3 * D)

        ps_agg = bank("ps_agg", 4)
        ps_t = bank("ps_t")
        ps_o = bank("ps_o")
        ps_l = bank("ps_l", 2)
        ps_nbr = [ps_l[:, 1, 0:D], ps_o[:, 0, 0:D]]
        ps_z = [ps_l[:, 0, 0:KD * P], ps_t[:, 0, 0:KD * P]]
        ps_logit = [ps_l[:, 0, KD * P:KD * P + E], ps_t[:, 0, KD * P:KD * P + E]]
        ps_h, ps_ht = ps_agg[:, 0:2, :], ps_agg[:, 2:4, :]

        x_in = [sem(f"x_in{g}") for g in range(NTG)]
        edges_in, wgt_in, small_in = sem("edges_in"), sem("wgt_in"), sem("small_in")
        w1_in, w2_in, b1_in, b2_in = sem("w1_in"), sem("w2_in"), sem("b1_in"), sem("b2_in")
        consts_ready = sem("consts_ready")
        dve_step, pool_step = sem("dve_step"), sem("pool_step")
        var_ready, std_ready = sem("var_ready"), sem("std_ready")
        rstd_ready, xn_by_act, xn_by_dve = sem("rstd_ready"), sem("xn_by_act"), sem("xn_by_dve")
        xn_out = [sem(f"xn_out{k}") for k in range(NXG)]
        least_ready, agg_zero = sem("least_ready"), sem("agg_zero")
        edge_tables, bad_summed, bad_ready = sem("edge_tables"), sem("bad_summed"), sem("bad_ready")
        gathered = [sem(f"gathered{k}") for k in range(2 * CG)]
        staged = [sem(f"staged{k}") for k in range(2)]
        s_ready, group_done, group_added = sem("s_ready"), sem("group_done"), sem("group_added")
        r_gathered = [sem(f"r_gathered{k}") for k in range(CG)]
        r_staged, r_s, r_done, r_added, r_shift = (
            sem("r_staged"), sem("r_s"), sem("r_done"), sem("r_added"), sem("r_shift"))
        own_norm, own_tr, own_copied, own_done, own_half, own_added = (
            sem("own_norm"), sem("own_tr"), sem("own_copied"), sem("own_done"), sem("own_half"), sem("own_added"))
        agg_copied, nbr_done = sem("agg_copied"), sem("nbr_done")
        x1_ready, x1_out, stat1, var1, std1, rstd1 = (
            sem("x1_ready"), sem("x1_out"), sem("stat1"), sem("var1"), sem("std1"), sem("rstd1"))
        z_ready, stat2, var2, std2, rstd2, zn_scale, zn_ready, zn_out = (
            sem("z_ready"), sem("stat2"), sem("var2"), sem("std2"), sem("rstd2"), sem("zn_scale"), sem("zn_ready"),
            sem("zn_out"))
        z_tr, z_copied, logit_done, logit_added = (
            sem("z_tr"), sem("z_copied"), sem("logit_done"), sem("logit_added"))
        carried, pool_carried = sem("carried"), sem("pool_carried")
        trash_zero, trash_out = sem("trash_zero"), sem("trash_out")
        shifted, exp_ready, masks_ready, shares_ready, ranks_ready = (
            sem("shifted"), sem("exp_ready"), sem("masks_ready"), sem("shares_ready"), sem("ranks_ready"))
        hot_eq, hot_weighed, hot_ready, hot_used, slots_ready = (
            sem("hot_eq"), sem("hot_weighed"), sem("hot_ready"), sem("hot_used"), sem("slots_ready"))
        first_tiles, tile_step, after_step, tiles_ready = (
            sem("first_tiles"), sem("tile_step"), sem("after_step"), sem("tiles_ready"))
        m_staged, m_sstaged = sem("m_staged"), sem("m_sstaged")
        m_gath = [sem(f"m_gath{k}") for k in range(4)]
        m_tr, m_xt, m_h, m_gelu, m_ht, m_htc, m_y, m_yw = (
            sem("m_tr"), sem("m_xt"), sem("m_h"), sem("m_gelu"), sem("m_ht"), sem("m_htc"), sem("m_y"), sem("m_yw"))
        m_sum, m_hb, m_yb = sem("m_sum"), sem("m_hb"), sem("m_yb")

        x_v = x.rearrange("(g t p) d -> g p t d", g=NTG, p=P)
        xn_v = xn_dram.rearrange("(g t p) d -> g p t d", g=NTG, p=P)

        block = ctx.enter_context(nc.Block())

        @block.sync
        def _(sp):
            sp.dma_start(dst_sb[:, :], dst_t).then_inc(edges_in, 16)
            sp.dma_start(first_sb[:, :], dst_first.to_broadcast([P, NG])).then_inc(edges_in, 16)
            for g in range(NTG):
                if g == 1:
                    sp.dma_start(wgt_sb, wgt_t).then_inc(wgt_in, 16)
                sp.dma_start(xs[:, g * TG * D:(g + 1) * TG * D].rearrange("p (t d) -> p t d", t=TG),
                             x_v[g]).then_inc(x_in[g], 16)
            sp.dma_start(wnbr_sb.rearrange("p (k n) -> p k n", k=KD),
                         w_nbr.rearrange("(k p) n -> p k n", p=P)).then_inc(small_in, 16)
            sp.dma_start(wown_sb.rearrange("p (k n) -> p k n", k=KD),
                         w_own.rearrange("(k p) n -> p k n", p=P)).then_inc(small_in, 16)
            sp.dma_start(bias_sb[:, :], bias.rearrange("(a n) -> a n", a=1).to_broadcast([P, D])
                         ).then_inc(small_in, 16)
            sp.dma_start(br_sb[:, :], br.rearrange("(a n) -> a n", a=1).to_broadcast([P, E])
                         ).then_inc(small_in, 16)
            sp.dma_start(wr_sb[:, :], Wr).then_inc(small_in, 16)
            sp.dma_start(lng_sb[:, :], ln_g).then_inc(small_in, 16)
            sp.dma_start(lnb_sb[:, :], ln_b).then_inc(small_in, 16)
            def stage(g, half):
                sp.dma_start(idx_stage[:, half * CG:(half + 1) * CG], src_t[:, ds(g * CG, CG)]
                             ).then_inc(staged[half], 16)

            stage(0, 0)
            stage(1, 1)
            for g in range(NTG):
                sp.wait_ge(xn_by_act, g + 1)
                sp.wait_ge(xn_by_dve, g + 1)
                sp.dma_start(xn_v[g], xg_stage[g % NXG].rearrange("p (t d) -> p t d", t=TG)
                             ).then_inc(xn_out[g % NXG], 16)
            sp.wait_ge(trash_zero, 1)
            sp.dma_start(ex_dram[TRASH:TRASH + P, :], y[:, 0:D]).then_inc(trash_out, 16)
            sp.dma_start(out[TRASH:TRASH + P, :], y[:, 0:D]).then_inc(trash_out, 16)

            def store(t, b=0):
                sp.wait_ge(x1_ready, t + 1)
                sp.dma_start(out[ds(t * P, P), :], xs[:, ds(t * D, D)]).then_inc(x1_out, 16)
                sp.wait_ge(zn_ready, t + 1)
                sp.dma_start(ex_dram[ds(t * P, P), :], zn[b]).then_inc(zn_out, 16)

            def iteration(i, chunks, tile):
                for half in range(2):
                    if chunks:
                        sp.wait_ge(group_done, 2 * i + half + 1)
                        stage(2 * i + 2 + half, half)
                    if tile and half == 0:
                        store(i - LAG)

            def weights_of(e):
                if not (isinstance(e, int) and e == 0):
                    sp.wait_ge(b1_in, 16 * e)
                sp.dma_start(b1_sb[:, ds(e * H, H)], b1[ds(e, 1), :].to_broadcast([P, H])).then_inc(b1_in, 16)
                if not (isinstance(e, int) and e == 0):
                    sp.wait_ge(w2_in, 16 * e)
                sp.dma_start(w2_sb[:, ds(e * (KH * D), KH * D)], W2[:, ds(e * (KH * D), KH * D)]).then_inc(w2_in, 16)

            with sp.Fori(0, LAG) as i:
                iteration(i, True, False)
            sp.dma_start(b2_sb[:, :], b2.rearrange("(a e) n -> a (e n)", a=1).to_broadcast([P, E * D])
                         ).then_inc(b2_in, 16)
            with sp.Fori(LAG, LAG + E * KD) as i:
                iteration(i, True, True)
                sp.dma_start(w1_sb[:, ds((i - LAG) * H, H)], W1[:, ds((i - LAG) * H, H)]).then_inc(w1_in, 16)
            with sp.Fori(LAG + E * KD, NIT - 1) as i:
                iteration(i, True, True)
            store(NIT - 1 - LAG)
            sp.wait_ge(gathered[2 * CG - 1], 16 * NIT)
            sp.wait_ge(x1_out, 16 * (NIT - LAG))
            for e in range(SOON):
                weights_of(e)

            for t in range(NIT - LAG, NT - 1):
                store(t)
            store(NT - 1, 1)
            sp.wait_ge(x1_out, 16 * NT)
            sp.wait_ge(zn_out, 16 * NT)
            sp.wait_ge(nbr_done, NT)
            sp.wait_ge(logit_done, NT)
            with sp.Fori(SOON, E - 2) as e:
                weights_of(e)
            sp.wait_ge(m_gath[3], 16)
            for e in range(E - 2, E):
                weights_of(e)
            sp.wait_ge(b1_in, 16 * E)
            sp.wait_ge(w2_in, 16 * E)
            sp.wait_ge(trash_out, 32)

        @block.gpsimd
        def _(pool):
            n = 0
            for t, v in ((ident, 0.0), (lower, 1.0), (ones, 1.0), (eps_sb, EPS)):
                pool.memset(t[:, :], v).then_inc(pool_step, 1)
                n += 1
            pool.memset(y[:, 0:D], 0.0).then_inc(trash_zero, 1)
            pool.wait_ge(pool_step, n)
            pool.affine_select(out=ident[:, :], in_=ident[:, :], compare_op=ALU.not_equal, fill=1.0, base=0,
                               pattern=[[-1, P]], channel_multiplier=1).then_inc(consts_ready, 1)
            pool.affine_select(out=lower[:, :], in_=lower[:, :], compare_op=ALU.is_ge, fill=0.0, base=-1,
                               pattern=[[1, P]], channel_multiplier=-1).then_inc(consts_ready, 1)
            pool.iota(iota_f[:, :], [[1, P]], base=0, channel_multiplier=0,
                      allow_small_or_imprecise_dtypes=True).then_inc(consts_ready, 1)
            pool.iota(iota_e[:, :], [[0, NT], [1, E]], base=0, channel_multiplier=0,
                      allow_small_or_imprecise_dtypes=True).then_inc(consts_ready, 1)
            pool.iota(iota_e8[:, :], [[0, NT], [1, E]], base=E, channel_multiplier=0,
                      allow_small_or_imprecise_dtypes=True).then_inc(consts_ready, 1)
            pool.iota(node_id[:, :], [[P, NT]], base=1, channel_multiplier=1,
                      allow_small_or_imprecise_dtypes=True).then_inc(consts_ready, 1)
            pool.iota(trash_id[:, :], [[1, 1]], base=TRASH + 1, channel_multiplier=1,
                      allow_small_or_imprecise_dtypes=True).then_inc(consts_ready, 1)

            pool.iota(early_g[:, NG:2 * NG], [[P, NIT], [0, 2]], base=(1 - LAG) * P, channel_multiplier=0,
                      allow_small_or_imprecise_dtypes=True).then_inc(least_ready, 1)
            pool.memset(agg_t, 0.0).then_inc(agg_zero, 1)

            def gather(to, at, done):
                pool.indirect_dma_start(out=to, out_offset=None, in_=xn_dram,
                                        in_offset=bass.IndirectOffsetOnAxis(ap=at, axis=0)).then_inc(done, 16)

            for k in range(NXG):
                pool.wait_ge(xn_out[k], 16 * len(range(k, NTG, NXG)))
            pool.wait_ge(bad_ready, 1)
            bad = pool.value_load(bad_i[0:1, 0:1], min_val=0, max_val=1)
            with pool.If(bad):
                with pool.Fori(0, NT) as w:
                    with pool.Fori(0, NG) as g:
                        pool.wait_ge(r_done, w * NG + g + 1)
                        pool.dma_start(r_stage[:, :], src_t[:, ds(g * CG, CG)]).then_inc(r_staged, 16)
                        pool.wait_ge(r_staged, w * (16 * NG) + g * 16 + 16)
                        pool.sem_inc(pool_carried, 1)
                        for k in range(CG):
                            gather(G[:, k * D:(k + 1) * D], r_stage[:, k:k + 1], r_gathered[k])
                pool.wait_ge(r_done, NT * NG + 1)

            def fetch(i):
                for half in range(2):
                    pool.wait_ge(staged[half], 16 * i + 16)
                    pool.sem_inc(pool_carried, 1)
                    for k in range(CG):
                        c = half * CG + k
                        gather(G[:, c * D:(c + 1) * D], idx_stage[:, c:c + 1], gathered[c])

            with pool.Fori(0, NIT) as i:
                fetch(i)

            pool.wait_ge(first_tiles, 1)
            pool.tensor_scalar(tile_of[:, :], iota_f[:, 0:MT], tbase[:, 1:2], None, ALU.is_ge).then_inc(tile_step, 1)
            for e in range(2, E):
                pool.wait_ge(tile_step, e - 1)
                pool.tensor_scalar(tile_after[:, e % 2 * MT:(e % 2 + 1) * MT], iota_f[:, 0:MT], tbase[:, e:e + 1],
                                   None, ALU.is_ge).then_inc(after_step, 1)
                pool.wait_ge(after_step, e - 1)
                pool.tensor_tensor(tile_of[:, :], tile_of[:, :], tile_after[:, e % 2 * MT:(e % 2 + 1) * MT], ALU.add
                                   ).then_inc(tile_step, 1)
            pool.wait_ge(tile_step, E - 1)
            pool.tensor_scalar(tile_used[:, :], iota_f[:, 0:MT], upto[:, E - 1:E], None, ALU.is_lt
                               ).then_inc(tiles_ready, 1)
            pool.tensor_scalar(last_tile[:, :], upto[:, E - 1:E], -1.0, None, ALU.add).then_inc(tiles_ready, 1)
            pool.tensor_copy(tile_ei[:, :], tile_of[:, :]).then_inc(tiles_ready, 1)
            pool.wait_ge(tiles_ready, 3)

            pool.wait_ge(slots_ready, 1)
            pool.wait_ge(zn_out, 16 * NT)
            pool.wait_ge(trash_out, 32)
            pool.wait_ge(x1_out, 16 * NT)

            def rows(a, k):
                if not (isinstance(a, int) and a < 4):
                    pool.wait_ge(m_tr, a - 3)
                pool.tensor_copy(gat_stage[:, k:k + 1], slot_idx[:, ds(a, 1)]).then_inc(m_staged, 1)
                pool.wait_ge(m_staged, a + 1)
                pool.sem_inc(pool_carried, 1)
                pool.indirect_dma_start(
                    out=xe[:, k * D:(k + 1) * D], out_offset=None, in_=ex_dram,
                    in_offset=bass.IndirectOffsetOnAxis(ap=gat_stage[:, k:k + 1], axis=0),
                ).then_inc(m_gath[k], 16)

            def add_rows(a, k, b):
                pool.tensor_copy(sca_stage[:, k:k + 1], slot_idx[:, ds(a, 1)]).then_inc(m_sstaged, 1)
                pool.wait_ge(m_sstaged, a + 1)
                pool.wait_ge(m_yw, a + 1)
                if not (isinstance(a, int) and a == 0):
                    pool.wait_ge(m_sum, 16 * a)
                pool.sem_inc(pool_carried, 1)
                pool.indirect_dma_start(
                    out=out, out_offset=bass.IndirectOffsetOnAxis(ap=sca_stage[:, k:k + 1], axis=0),
                    in_=y[:, b * D:(b + 1) * D], in_offset=None, compute_op=ALU.add,
                ).then_inc(m_sum, 16)

            def used(a):
                return pool.value_load(tile_used[0:1, a:a + 1], min_val=0, max_val=1)

            for a in range(4):
                rows(a, a)
            for a in range(4):
                rows(a + 4, a)
                add_rows(a, a % 2, a % 2)
            with pool.Fori(1, SURE // 4 - 1) as i:
                for k in range(4):
                    rows(4 * i + (k + 4), k)
                    add_rows(4 * i + k, k % 2, k % 2)
            for a in range(SURE - 4, MT):
                if a + 4 < MT:
                    with pool.If(used(a + 4)):
                        rows(a + 4, a % 4)
                if a < SURE:
                    add_rows(a, a % 2, 2 if a == SURE - 1 else a % 2)
                else:
                    with pool.If(used(a)):
                        add_rows(a, a % 2, 2)
            pool.wait_ge(m_sum, 16 * pool.value_load(last_tile[0:1, 0:1], min_val=SURE, max_val=MT - 1) + 16)

        @block.vector
        def _(dve):
            steps = [0]

            def step(ins):
                steps[0] += 1
                ins.then_inc(dve_step, 1)
                dve.wait_ge(dve_step, steps[0])

            def row_stats(g):
                dve.wait_ge(x_in[g], 16)
                o = g % 2 * TG * 6
                for t in range(TG):
                    last = dve.bn_stats(stat[:, o + t * 6:o + t * 6 + 6],
                                        xs[:, (g * TG + t) * D:(g * TG + t + 1) * D])
                step(last)
                for t in range(TG):
                    last = dve.bn_aggr(mv[:, 2 * (g * TG + t):2 * (g * TG + t) + 2], stat[:, o + t * 6:o + t * 6 + 6])
                last.then_inc(var_ready, 1)

            row_stats(0)
            for g in range(NTG):
                if g + 1 < NTG:
                    if g:
                        dve.wait_ge(var_ready, g)
                    row_stats(g + 1)
                dve.wait_ge(std_ready, g + 1)
                at = slice(g * TG, (g + 1) * TG)
                step(dve.reciprocal(rstd[:, at], rstd[:, at]))
                dve.scalar_tensor_tensor(out=nmr_x[:, at], in0=mv[:, 2 * g * TG:2 * (g + 1) * TG:2], scalar=-1.0,
                                         in1=rstd[:, at], op0=ALU.mult, op1=ALU.mult).then_inc(rstd_ready, 1)
                if g >= NXG:
                    dve.wait_ge(xn_out[g % NXG], 16 * (g // NXG))
                for t in range(BY_ACT, TG):
                    c = g * TG + t
                    last = dve.tensor_scalar(xg_stage[g % NXG][:, t * D:(t + 1) * D], xs[:, c * D:(c + 1) * D],
                                             mv[:, 2 * c:2 * c + 1], rstd[:, c:c + 1], ALU.subtract, ALU.mult)
                last.then_inc(xn_by_dve, 1)

            dve.wait_ge(edges_in, 32)
            step(dve.tensor_tensor(rel.rearrange("p (g k) -> p g k", k=CG),
                                   dst_sb[:, :].rearrange("p (g k) -> p g k", k=CG),
                                   first_sb[:, :].rearrange("p (g k) -> p g k", k=1).to_broadcast([P, NG, CG]),
                                   ALU.subtract))
            dve.tensor_scalar(inside, rel, 0.0, None, ALU.is_ge)
            step(dve.tensor_scalar(rest, rel, float(P), None, ALU.is_lt))
            step(dve.tensor_tensor(inside, inside, rest, ALU.mult))
            dve.tensor_copy(rest, dst_sb[:, :])
            dve.tensor_reduce(n_bad[:, 0:1], inside, AX.X, ALU.add)
            dve.wait_ge(consts_ready, 7)
            dve.wait_ge(least_ready, 1)
            step(dve.tensor_tensor(early_g[:, 0:NG], first_sb[:, :], early_g[:, NG:2 * NG], ALU.is_ge))
            step(dve.tensor_reduce(n_bad[:, 1:2], early_g[:, 0:NG], AX.X, ALU.add))
            step(dve.tensor_tensor(n_bad[:, 0:1], n_bad[:, 0:1], n_bad[:, 1:2], ALU.add))
            dve.tensor_scalar(n_bad[:, 2:3], n_bad[:, 0:1], -1.0, float(NCH + NG), ALU.mult, ALU.add
                              ).then_inc(edge_tables, 1)
            dve.wait_ge(bad_summed, 1)
            dve.tensor_scalar(good[:, :], ps_l[:, 0, 0:1], 0.0, None, ALU.is_equal)
            step(dve.tensor_scalar(bad_i[:, :], ps_l[:, 0, 0:1], 1.0, None, ALU.min))
            dve.sem_inc(bad_ready, 1)

            dve.wait_ge(small_in, 7 * 16)
            dve.wait_ge(wgt_in, 16)
            dve.wait_ge(agg_zero, 1)

            def one_hots(table, c0, half, done):
                for k in range(CG):
                    s = half * CG + k
                    last = dve.tensor_scalar(S[:, s * P:(s + 1) * P], iota_f[:, :], table[:, ds(c0 + k, 1)],
                                             wgt_sb[:, ds(c0 + k, 1)], ALU.is_equal, ALU.mult)
                last.then_inc(done, 1)

            def sums(base, half, done):
                dve.tensor_tensor(agg_v[:, :, ds(base, P)], agg_v[:, :, ds(base, P)],
                                  ps_agg[:, 2 * half:2 * half + 2, 0:P], ALU.add).then_inc(done, 1)

            bad = dve.value_load(bad_i[0:1, 0:1], min_val=0, max_val=1)
            with dve.If(bad):
                dve.sem_inc(r_added, 1)
                dve.sem_inc(r_shift, 1)
                with dve.Fori(0, NT) as w:
                    with dve.Fori(0, NG) as g:
                        dve.wait_ge(r_done, w * NG + g + 1)
                        dve.wait_ge(r_shift, w + 1)
                        one_hots(rest, g * CG, 0, r_s)
                        dve.wait_ge(r_done, w * NG + g + 2)
                        dve.wait_ge(r_added, w * NG + g + 1)
                        sums(w * P, 0, r_added)
                    dve.tensor_scalar(rest, rest, float(-P), None, ALU.add).then_inc(r_shift, 1)
                dve.wait_ge(r_added, NT * NG + 1)
            dve.tensor_scalar(wgt_sb, wgt_sb, good[:, 0:1], None, ALU.mult)
            step(dve.tensor_scalar(first_sb[:, :], first_sb[:, :], float(-NROW), good[:, 0:1], ALU.add, ALU.mult))
            step(dve.tensor_scalar(first_sb[:, :], first_sb[:, :], float(NROW), None, ALU.add))

            def te(t):
                return t.rearrange("p (t e) -> p t e", e=E)

            m1, m2 = both_masks[:, 0:NT * E], both_masks[:, NT * E:2 * NT * E]

            def route(t0, n, done):
                cut_t, cut_e = slice(t0, t0 + n), slice(t0 * E, (t0 + n) * E)

                def over_e(v):
                    return v[:, cut_t].rearrange("p (t a) -> p t a", a=1).to_broadcast([P, n, E])

                def part(v):
                    return te(v[:, cut_e])

                dve.wait_ge(logit_added, t0 + n)
                step(dve.tensor_reduce(mx[:, cut_t], part(logit), AX.X, ALU.max))
                dve.tensor_tensor(part(logit_less), part(logit), over_e(mx), ALU.subtract).then_inc(shifted, 1)
                dve.wait_ge(exp_ready, done + 1)
                step(dve.tensor_reduce(sm[:, cut_t], part(expo), AX.X, ALU.add))
                step(dve.reciprocal(sm[:, cut_t], sm[:, cut_t]))
                step(dve.tensor_tensor(part(probs), part(expo), over_e(sm), ALU.mult))
                for mask, best, at in ((m1, p1, i1), (m2, p2, i2)):
                    step(dve.tensor_reduce(best[:, cut_t], part(probs), AX.X, ALU.max))
                    step(dve.tensor_tensor(part(is_best), part(probs), over_e(best), ALU.is_equal))
                    step(dve.scalar_tensor_tensor(out=work[:, cut_e], in0=is_best[:, cut_e], scalar=float(-E),
                                                  in1=iota_e8[:, cut_e], op0=ALU.mult, op1=ALU.add))
                    step(dve.tensor_reduce(at[:, cut_t], part(work), AX.X, ALU.min))
                    step(dve.tensor_tensor(part(mask), part(iota_e), over_e(at), ALU.is_equal))
                    if mask is m1:
                        step(dve.scalar_tensor_tensor(out=probs[:, cut_e], in0=mask[:, cut_e], scalar=-2.0,
                                                      in1=probs[:, cut_e], op0=ALU.mult, op1=ALU.add))
                dve.tensor_tensor(chosen.rearrange("p (e t) -> p t e", e=E)[:, cut_t, :], part(m1), part(m2), ALU.add
                                  ).then_inc(masks_ready, 1)

            def own_norm_of(t):
                if not (isinstance(t, int) and t == 0):
                    dve.wait_ge(own_tr, t)
                dve.tensor_scalar(one_tile, xs[:, ds(t * D, D)], mv[:, ds(2 * t, 1)], rstd[:, ds(t, 1)],
                                  ALU.subtract, ALU.mult).then_inc(own_norm, 1)

            def own_add_of(t):
                at = xs[:, ds(t * D, D)]
                dve.wait_ge(own_done, t + 1)
                dve.tensor_tensor(at, at, ps_o[:, 0, 0:D], ALU.add).then_inc(own_half, 1)
                dve.wait_ge(own_half, t + 1)
                dve.tensor_tensor(at, at, bias_sb[:, :], ALU.add).then_inc(own_added, 1)

            def x1_of(t, b=0):
                at = xs[:, ds(t * D, D)]
                dve.wait_ge(own_added, t + 1)
                dve.wait_ge(nbr_done, t + 1)
                dve.tensor_tensor(at, at, ps_nbr[b], ALU.add).then_inc(x1_ready, 1)
                dve.wait_ge(x1_ready, t + 1)
                dve.sem_inc(carried, 1)
                dve.bn_stats(stat[:, 12 * b:12 * b + 6], at).then_inc(stat1, 1)
                dve.wait_ge(stat1, t + 1)
                dve.sem_inc(carried, 1)
                dve.bn_aggr(mv2[b][:, 0:2], stat[:, 12 * b:12 * b + 6]).then_inc(var1, 1)

            def z_of(t, b=0):
                dve.wait_ge(std1, t + 1)
                dve.reciprocal(rs2[b][:, 0:1], rs2[b][:, 0:1]).then_inc(rstd1, 1)
                dve.wait_ge(rstd1, t + 1)
                if not (isinstance(t, int) and t == 0) and b == 0:
                    dve.wait_ge(z_tr, t)
                    dve.wait_ge(zn_ready, t)
                dve.tensor_scalar(zt[b], xs[:, ds(t * D, D)], mv2[b][:, 0:1], rs2[b][:, 0:1],
                                  ALU.subtract, ALU.mult).then_inc(z_ready, 1)
                dve.wait_ge(z_ready, t + 1)
                dve.sem_inc(carried, 1)
                dve.bn_stats(stat[:, 12 * b + 6:12 * b + 12], zt[b]).then_inc(stat2, 1)
                dve.wait_ge(stat2, t + 1)
                dve.sem_inc(carried, 1)
                dve.bn_aggr(mv2[b][:, 2:4], stat[:, 12 * b + 6:12 * b + 12]).then_inc(var2, 1)

            def zn_scale_of(t, b=0):
                dve.wait_ge(std2, t + 1)
                dve.reciprocal(rs2[b][:, 1:2], rs2[b][:, 1:2]).then_inc(rstd2, 1)
                dve.wait_ge(rstd2, t + 1)
                dve.scalar_tensor_tensor(out=nmr[b][:, :], in0=mv2[b][:, 2:3], scalar=-1.0, in1=rs2[b][:, 1:2],
                                         op0=ALU.mult, op1=ALU.mult).then_inc(zn_scale, 1)

            def logits_of(t, b=0):
                dve.wait_ge(logit_done, t + 1)
                dve.tensor_tensor(logit[:, ds(t * E, E)], ps_logit[b], br_sb[:, :], ALU.add
                                  ).then_inc(logit_added, 1)

            def add_group(i, half):
                g = 2 * i + half
                base = dve.value_load(first_sb[0:1, ds(g, 1)], min_val=0, max_val=NROW)
                dve.wait_ge(group_done, g + 1)
                if not (isinstance(g, int) and g == 0):
                    dve.wait_ge(group_added, g)
                sums(base, half, group_added)

            def iteration(i, own, chunks, more, tile):
                if own:
                    own_norm_of(i)
                if chunks:
                    add_group(i, 0)
                if more:
                    one_hots(rel, (i + 1) * (2 * CG), 0, s_ready)
                if tile:
                    x1_of(i - LAG)
                    z_of(i - LAG)
                    zn_scale_of(i - LAG)
                if chunks:
                    add_group(i, 1)
                if more:
                    one_hots(rel, (i + 1) * (2 * CG) + CG, 1, s_ready)
                if own:
                    own_add_of(i)
                if tile:
                    logits_of(i - LAG)

            for half in range(2):
                one_hots(rel, half * CG, half, s_ready)
            iteration(0, True, True, True, False)
            with dve.Fori(1, LAG) as i:
                iteration(i, True, True, True, False)
            iteration(LAG, True, True, True, True)
            with dve.Fori(LAG + 1, NT) as i:
                iteration(i, True, True, True, True)
            with dve.Fori(NT, NIT - 1) as i:
                iteration(i, False, True, True, True)
            step(dve.tensor_scalar(valid[:, :], node_id[:, :], float(N), None, ALU.is_le))
            step(dve.tensor_tensor(tokv[:, :], node_id[:, :], valid[:, :], ALU.mult))
            step(dve.tensor_scalar(mx[:, :], valid[:, :], -1000.0, 1000.0, ALU.mult, ALU.add))
            step(dve.tensor_tensor(te(iota_e8[:, :]), te(iota_e8[:, :]),
                                   mx[:, :].rearrange("p (t a) -> p t a", a=1).to_broadcast([P, NT, E]), ALU.add))
            step(dve.memset(ones_te[:, :], 1.0))
            route(0, FIRST, 0)
            iteration(NIT - 1, False, True, False, True)
            for stage in (x1_of, z_of, zn_scale_of, logits_of):
                for k in range(2):
                    stage(NT - 2 + k, k)

            route(FIRST, NT - FIRST, 1)
            step(dve.tensor_tensor(sm[:, :], p1[:, :], p2[:, :], ALU.add))
            step(dve.reciprocal(sm[:, :], sm[:, :]))
            step(dve.tensor_tensor(sm[:, :], sm[:, :], valid[:, :], ALU.mult))
            dve.tensor_tensor(w1v[:, :], p1[:, :], sm[:, :], ALU.mult)
            dve.tensor_tensor(w2v[:, :], p2[:, :], sm[:, :], ALU.mult).then_inc(shares_ready, 1)

            dve.wait_ge(ranks_ready, 1)
            columns = ps_l[:, 1, 0:NT * E]
            step(dve.tensor_tensor_scan(slots, ones_te[:, :], columns, 0.0, ALU.mult, ALU.add))
            step(dve.tensor_tensor(work, slots, columns, ALU.subtract))
            start = work.rearrange("p (e t) -> p e t", e=E)[:, :, 0]
            upto_last = slots.rearrange("p (e t) -> p e t", e=E)[:, :, NT - 1]
            step(dve.tensor_tensor(cnt[:, :], upto_last, start, ALU.subtract))
            step(dve.tensor_scalar(cnt_i[:, 0:E], cnt[:, :], float(P - 1), None, ALU.add))
            step(dve.tensor_scalar(cnt_i[:, E:2 * E], cnt_i[:, 0:E], 7, None, ALU.arith_shift_right))
            step(dve.tensor_copy(tiles[:, :], cnt_i[:, E:2 * E]))
            step(dve.tensor_tensor_scan(upto[:, :], ones_te[:, 0:E], tiles[:, :], 0.0, ALU.mult, ALU.add))
            step(dve.tensor_tensor(tbase[:, :], upto[:, :], tiles[:, :], ALU.subtract))
            dve.sem_inc(first_tiles, 1)
            step(dve.scalar_tensor_tensor(out=off[:, :], in0=tbase[:, :], scalar=float(P), in1=start,
                                          op0=ALU.mult, op1=ALU.subtract))
            step(dve.tensor_tensor(work, work, ps_l[:, 0, 0:NT * E], ALU.add))
            step(dve.tensor_tensor(te(slots), work.rearrange("p (e t) -> p t e", e=E),
                                   off[:, :].rearrange("p (a e) -> p a e", a=1).to_broadcast([P, NT, E]), ALU.add))
            step(dve.tensor_tensor(both_masks[:, :].rearrange("p (k c) -> p k c", k=2),
                                   both_masks[:, :].rearrange("p (k c) -> p k c", k=2),
                                   slots.rearrange("p (a c) -> p a c", a=1).to_broadcast([P, 2, NT * E]), ALU.mult))
            step(dve.tensor_reduce(slot_f[:, :], te(both_masks[:, :]), AX.X, ALU.add))
            step(dve.tensor_copy(slot_i[:, :], slot_f[:, :]))
            dve.tensor_scalar(part_i[:, 0:2 * NT], slot_i[:, :], 7, None, ALU.arith_shift_right)
            step(dve.tensor_scalar(part_i[:, 2 * NT:4 * NT], slot_i[:, :], P - 1, None, ALU.bitwise_and))
            step(dve.tensor_copy(place[:, :], part_i[:, :]))

            def per_tile(v, t0, n):
                return v[:, ds(t0, TG)].rearrange("p (t a) -> p t a", a=1).to_broadcast([P, TG, n])

            def iotas(n):
                return iota_f[:, 0:n].rearrange("p (a n) -> p a n", a=1).to_broadcast([P, TG, n])

            def slots_of(g, first):
                for k in range(2):
                    if not first:
                        dve.wait_ge(hot_used, 2 * g + k - 1)
                    rows3 = hot_row[:, k * TG * P:(k + 1) * TG * P].rearrange("p (t n) -> p t n", t=TG)
                    both = hot_tile[:, 2 * k * TG * MT:2 * (k + 1) * TG * MT].rearrange(
                        "p (t a n) -> p t a n", t=TG, a=2)
                    one3 = hot_one[:, k * TG * MT:(k + 1) * TG * MT].rearrange("p (t n) -> p t n", t=TG)
                    dve.tensor_tensor(one3, iotas(MT), per_tile(place, g * TG + k * NT, MT), ALU.is_equal
                                      ).then_inc(hot_eq, 1)
                    dve.tensor_tensor(rows3, iotas(P), per_tile(place, g * TG + (2 + k) * NT, P), ALU.is_equal)
                    dve.wait_ge(hot_eq, 2 * g + k + 1)
                    dve.tensor_tensor(both[:, :, 0, :], one3, per_tile(tokv, g * TG, MT), ALU.mult
                                      ).then_inc(hot_ready, 1)

            slots_of(0, True)
            with dve.Fori(1, NTG) as g:
                slots_of(g, False)
            dve.wait_ge(hot_used, 2 * NTG)
            step(dve.tensor_copy(tok[:, :], ps_o[:, 0, 0:2 * MT]))
            step(dve.tensor_scalar(tile_e[:, :], tok[:, 0:MT], 0.0, trash_id[:, :], ALU.is_equal, ALU.mult))
            step(dve.scalar_tensor_tensor(out=tile_e[:, :], in0=tile_e[:, :], scalar=-1.0, in1=tok[:, 0:MT],
                                          op0=ALU.add, op1=ALU.add))
            dve.tensor_copy(slot_idx[:, :], tile_e[:, :]).then_inc(slots_ready, 1)

            def expert(a):
                return dve.value_load(tile_ei[0:1, ds(a, 1)], min_val=0, max_val=E - 1)

            def add_b1(a):
                e = expert(a)
                dve.wait_ge(b1_in, e * 16 + 16)
                for n in range(2):
                    dve.wait_ge(m_h, 2 * a + n + 1)
                    if n == 0 and not (isinstance(a, int) and a == 0):
                        dve.wait_ge(m_ht, 2 * a)
                    dve.tensor_tensor(hid[:, n * 512:(n + 1) * 512], ps_h[:, n, :],
                                      b1_sb[:, ds(e * H + n * 512, 512)], ALU.add).then_inc(m_hb, 1)

            def hidden_copy(a):
                for n in range(2):
                    dve.wait_ge(m_ht, 2 * a + n + 1)
                    if n == 0 and not (isinstance(a, int) and a == 0):
                        dve.wait_ge(m_y, a)
                    dve.tensor_copy(hid_t[:, n * 512:(n + 1) * 512], ps_ht[:, n, :]).then_inc(m_htc, 1)

            def weigh(a, k):
                at = y[:, k * D:(k + 1) * D]
                e = expert(a)
                dve.wait_ge(m_y, a + 1)
                if not (isinstance(a, int) and a < 2):
                    dve.wait_ge(m_sum, 16 * a if k == 2 else 16 * a - 16)
                dve.tensor_tensor(at, ps_o[:, 0, 0:D], b2_sb[:, ds(e * D, D)], ALU.add).then_inc(m_yb, 1)
                dve.wait_ge(m_yb, a + 1)
                dve.tensor_scalar(at, at, tok[:, ds(a + MT, 1)], None, ALU.mult).then_inc(m_yw, 1)

            def used(a):
                return dve.value_load(tile_used[0:1, a:a + 1], min_val=0, max_val=1)

            dve.wait_ge(tiles_ready, 3)
            dve.wait_ge(trash_out, 32)
            dve.wait_ge(b2_in, 16)
            add_b1(0)
            hidden_copy(0)
            add_b1(1)
            weigh(0, 0)
            hidden_copy(1)
            with dve.Fori(1, SURE // 2) as i:
                for k in range(2):
                    add_b1(2 * i + k)
                    weigh(2 * i + (k - 1), (k + 1) % 2)
                    hidden_copy(2 * i + k)
            for a in range(SURE, MT):
                with dve.If(used(a)):
                    add_b1(a)
                    weigh(a - 1, 2)
                    hidden_copy(a)
            weigh(dve.value_load(last_tile[0:1, 0:1], min_val=SURE, max_val=MT - 1), 2)

        @block.scalar
        def _(act):
            act.wait_ge(consts_ready, 1)
            act.activation(rs2[0][:, 0:1], eps_sb[:, :], ACT.Sqrt)

            def std(g):
                act.wait_ge(var_ready, g + 1)
                v = mv[:, 2 * g * TG:2 * (g + 1) * TG]
                act.activation(rstd[:, g * TG:(g + 1) * TG], v[:, 1:2 * TG:2], ACT.Sqrt, bias=eps_sb[:, :]
                               ).then_inc(std_ready, 1)

            std(0)
            for g in range(NTG):
                if g + 1 < NTG:
                    std(g + 1)
                act.wait_ge(rstd_ready, g + 1)
                if g >= NXG:
                    act.wait_ge(xn_out[g % NXG], 16 * (g // NXG))
                for t in range(BY_ACT):
                    c = g * TG + t
                    last = act.activation(xg_stage[g % NXG][:, t * D:(t + 1) * D], xs[:, c * D:(c + 1) * D],
                                          ACT.Identity, bias=nmr_x[:, c:c + 1], scale=rstd[:, c:c + 1])
                last.then_inc(xn_by_act, 1)

            def agg_copy(t, whole, b=0):
                if not (isinstance(t, int) and t == 0) and b == 0:
                    act.wait_ge(nbr_done, t)
                act.wait_ge(group_added, whole)
                act.activation(agg_in[b].rearrange("p (k n) -> p k n", k=KD),
                               agg_v[:, :, ds(t * P, P)], ACT.Copy).then_inc(agg_copied, 1)

            def own_copy(t):
                if not (isinstance(t, int) and t == 0):
                    act.wait_ge(own_done, t)
                act.wait_ge(own_tr, t + 1)
                act.activation(own_t, ps_t[:, 0, 0:KD * P], ACT.Copy).then_inc(own_copied, 1)

            def z_std(t, b=0):
                act.wait_ge(var1, t + 1)
                act.activation(rs2[b][:, 0:1], mv2[b][:, 1:2], ACT.Sqrt, bias=eps_sb[:, :]).then_inc(std1, 1)

            def zn_std(t, b=0):
                act.wait_ge(var2, t + 1)
                act.activation(rs2[b][:, 1:2], mv2[b][:, 3:4], ACT.Sqrt, bias=eps_sb[:, :]).then_inc(std2, 1)

            def zn_of(t, b=0):
                act.wait_ge(zn_scale, t + 1)
                if not (isinstance(t, int) and t == 0) and b == 0:
                    act.wait_ge(zn_out, 16 * t)
                act.activation(zn[b], zt[b], ACT.Identity, bias=nmr[b][:, 0:1], scale=rs2[b][:, 1:2]
                               ).then_inc(zn_ready, 1)

            def z_copy(t, b=0):
                act.wait_ge(z_tr, t + 1)
                if not (isinstance(t, int) and t == 0) and b == 0:
                    act.wait_ge(logit_done, t)
                act.activation(z_t[b], ps_z[b], ACT.Copy).then_inc(z_copied, 1)

            def exps(c0, c1, done):
                act.wait_ge(shifted, done + 1)
                act.activation(expo[:, c0:c1], logit_less[:, c0:c1], ACT.Exp).then_inc(exp_ready, 1)

            def iteration(i, own, tile, whole):
                if tile:
                    agg_copy(i - LAG, whole)
                if own:
                    own_copy(i)
                if tile:
                    for stage in (z_std, zn_std, zn_of, z_copy):
                        stage(i - LAG)

            iteration(0, True, False, None)
            with act.Fori(1, LAG) as i:
                iteration(i, True, False, None)
            iteration(LAG, True, True, 2 * LAG)
            with act.Fori(LAG + 1, NT) as i:
                iteration(i, True, True, 2 * i)
            with act.Fori(NT, NIT - 1) as i:
                iteration(i, False, True, 2 * i)
            exps(0, FIRST * E, 0)
            iteration(NIT - 1, False, True, 2 * NIT - 2)
            for k in range(2):
                agg_copy(NT - 2 + k, NG, k)
            for stage in (z_std, zn_std, zn_of, z_copy):
                for k in range(2):
                    stage(NT - 2 + k, k)

            exps(FIRST * E, NT * E, 1)

            def slot_weights(g, first):
                for k in range(2):
                    act.wait_ge(hot_eq, 2 * g + k + 1)
                    if not first:
                        act.wait_ge(hot_used, 2 * g + k - 1)
                    for j in range(TG):
                        c = k * TG + j
                        last = act.activation(hot_tile[:, (2 * c + 1) * MT:(2 * c + 2) * MT],
                                              hot_one[:, c * MT:(c + 1) * MT], ACT.Copy,
                                              scale=(w1v, w2v)[k][:, ds(g * TG + j, 1)])
                    last.then_inc(hot_weighed, 1)

            act.wait_ge(shares_ready, 1)
            slot_weights(0, True)
            with act.Fori(1, NTG) as g:
                slot_weights(g, False)

            act.activation(nmr[0][:, :], eps_sb[:, :], ACT.Gelu)
            act.wait_ge(tiles_ready, 3)

            def scaled(a, k):
                e = act.value_load(tile_ei[0:1, ds(a, 1)], min_val=0, max_val=E - 1)
                act.wait_ge(m_tr, a + 1)
                if not (isinstance(a, int) and a < 2):
                    act.wait_ge(m_h, 2 * a - 2)
                for d in range(KD):
                    last = act.activation(xe_t[:, (k * KD + d) * P:(k * KD + d + 1) * P],
                                          ps_t[:, 0, d * P:(d + 1) * P], ACT.Identity,
                                          bias=lnb_sb[:, ds(e + d * E, 1)], scale=lng_sb[:, ds(e + d * E, 1)])
                last.then_inc(m_xt, 1)

            def gelu(a):
                for n in range(2):
                    act.wait_ge(m_hb, 2 * a + n + 1)
                    half = hid[:, n * 512:(n + 1) * 512]
                    act.activation(half, half, ACT.Gelu).then_inc(m_gelu, 1)

            def used(a):
                return act.value_load(tile_used[0:1, a:a + 1], min_val=0, max_val=1)

            scaled(0, 0)
            scaled(1, 1)
            gelu(0)
            with act.Fori(1, SURE // 2) as i:
                scaled(2 * i, 0)
                gelu(2 * i - 1)
                scaled(2 * i + 1, 1)
                gelu(2 * i)
            for a in range(SURE, MT):
                with act.If(used(a)):
                    scaled(a, a % 2)
                    gelu(a - 1)
            gelu(act.value_load(last_tile[0:1, 0:1], min_val=SURE, max_val=MT - 1))

        @block.tensor
        def _(pe):
            pe.wait_ge(edge_tables, 1)
            pe.wait_ge(consts_ready, 7)
            pe.matmul(ps_l[:, 0, 0:1], ones[:, :], n_bad[:, 2:3], start=True, stop=True).then_inc(bad_summed, 1)
            pe.wait_ge(small_in, 7 * 16)

            def products(half, rows_in, count, ready, count_s, free, count_f, done):
                for k in range(CG):
                    s = half * CG + k
                    pe.wait_ge(rows_in[s], count)
                    if k == 0:
                        pe.wait_ge(ready, count_s)
                        if count_f is not None:
                            pe.wait_ge(free, count_f)
                    for d in range(KD):
                        last = pe.matmul(ps_agg[:, 2 * half + d, 0:P], G[:, s * D + d * P:s * D + (d + 1) * P],
                                         S[:, s * P:(s + 1) * P], start=(k == 0), stop=(k == CG - 1))
                last.then_inc(done, 1)

            pe.wait_ge(bad_ready, 1)
            bad = pe.value_load(bad_i[0:1, 0:1], min_val=0, max_val=1)
            with pe.If(bad):
                pe.sem_inc(r_done, 1)
                with pe.Fori(0, NT) as w:
                    with pe.Fori(0, NG) as g:
                        products(0, r_gathered, w * (16 * NG) + g * 16 + 16, r_s, w * NG + g + 1,
                                 r_added, w * NG + g + 1, r_done)
                pe.wait_ge(r_added, NT * NG + 1)

            def group(i, half):
                first = isinstance(i, int) and i == 0
                products(half, gathered, 16 * i + 16, s_ready, 2 * i + half + 1,
                         group_added, None if first else 2 * i + half - 1, group_done)

            def own_transpose(t):
                pe.wait_ge(own_norm, t + 1)
                if not (isinstance(t, int) and t == 0):
                    pe.wait_ge(own_copied, t)
                for d in range(KD):
                    last = pe.transpose(ps_t[:, 0, d * P:(d + 1) * P], one_tile[:, d * P:(d + 1) * P], ident[:, :])
                last.then_inc(own_tr, 1)

            def own_product(t):
                pe.wait_ge(own_copied, t + 1)
                if not (isinstance(t, int) and t == 0):
                    pe.wait_ge(own_half, t)
                for d in range(KD):
                    last = pe.matmul(ps_o[:, 0, 0:D], own_t[:, d * P:(d + 1) * P],
                                     wown_sb[:, d * D:(d + 1) * D], start=(d == 0), stop=(d == KD - 1))
                last.then_inc(own_done, 1)

            def nbr_product(t, b=0):
                pe.wait_ge(agg_copied, t + 1)
                if not (isinstance(t, int) and t == 0) and b == 0:
                    pe.wait_ge(x1_ready, t)
                for d in range(KD):
                    last = pe.matmul(ps_nbr[b], agg_in[b][:, d * P:(d + 1) * P],
                                     wnbr_sb[:, d * D:(d + 1) * D], start=(d == 0), stop=(d == KD - 1))
                last.then_inc(nbr_done, 1)

            def z_transpose(t, b=0):
                pe.wait_ge(z_ready, t + 1)
                if not (isinstance(t, int) and t == 0) and b == 0:
                    pe.wait_ge(z_copied, t)
                for d in range(KD):
                    last = pe.transpose(ps_z[b][:, d * P:(d + 1) * P], zt[b][:, d * P:(d + 1) * P], ident[:, :])
                last.then_inc(z_tr, 1)

            def logits_of(t, b=0):
                pe.wait_ge(z_copied, t + 1)
                if not (isinstance(t, int) and t == 0) and b == 0:
                    pe.wait_ge(logit_added, t)
                for d in range(KD):
                    last = pe.matmul(ps_logit[b], z_t[b][:, d * P:(d + 1) * P],
                                     wr_sb[:, d * E:(d + 1) * E], start=(d == 0), stop=(d == KD - 1))
                last.then_inc(logit_done, 1)

            def iteration(i, own, chunks, tile):
                if chunks:
                    group(i, 0)
                if own:
                    own_transpose(i)
                if tile:
                    nbr_product(i - LAG)
                if chunks:
                    group(i, 1)
                if own:
                    own_product(i)
                if tile:
                    z_transpose(i - LAG)
                    logits_of(i - LAG)

            iteration(0, True, True, False)
            with pe.Fori(1, LAG) as i:
                iteration(i, True, True, False)
            iteration(LAG, True, True, True)
            with pe.Fori(LAG + 1, NT) as i:
                iteration(i, True, True, True)
            with pe.Fori(NT, NIT) as i:
                iteration(i, False, True, True)
            pe.wait_ge(own_half, NT)
            pe.wait_ge(own_copied, NT)
            for stage in (nbr_product, z_transpose, logits_of):
                for k in range(2):
                    stage(NT - 2 + k, k)

            pe.wait_ge(masks_ready, 2)
            pe.matmul(ps_l[:, 0, 0:NT * E], lower[:, :], chosen, start=True, stop=True)
            pe.matmul(ps_l[:, 1, 0:NT * E], ones[:, :], chosen, start=True, stop=True).then_inc(ranks_ready, 1)

            def slots_of(g, first, final):
                for k in range(2):
                    pe.wait_ge(hot_ready, 2 * g + k + 1)
                    pe.wait_ge(hot_weighed, 2 * g + k + 1)
                    for j in range(TG):
                        c = k * TG + j
                        last = pe.matmul(ps_o[:, 0, 0:2 * MT], hot_row[:, c * P:(c + 1) * P],
                                         hot_tile[:, c * 2 * MT:(c + 1) * 2 * MT], start=(first and c == 0),
                                         stop=(final and c == 2 * TG - 1), skip_group_check=True)
                    last.then_inc(hot_used, 1)

            pe.wait_ge(x1_ready, NT)
            slots_of(0, True, False)
            with pe.Fori(1, NTG - 1) as g:
                slots_of(g, False, False)
            slots_of(NTG - 1, False, True)

            pe.wait_ge(tiles_ready, 3)
            pe.wait_ge(w1_in, 16 * E * KD)

            def expert(a):
                return pe.value_load(tile_ei[0:1, ds(a, 1)], min_val=0, max_val=E - 1)

            def used(a):
                return pe.value_load(tile_used[0:1, a:a + 1], min_val=0, max_val=1)

            def rows_t(a, k, n):
                pe.wait_ge(m_gath[k], n)
                if not (isinstance(a, int) and a == 0):
                    pe.wait_ge(m_xt, a)
                for d in range(KD):
                    last = pe.transpose(ps_t[:, 0, d * P:(d + 1) * P], xe[:, k * D + d * P:k * D + (d + 1) * P],
                                        ident[:, :])
                last.then_inc(m_tr, 1)

            def layer1(a, k, e):
                pe.wait_ge(m_xt, a + 1)
                for n in range(2):
                    if not (isinstance(a, int) and a == 0):
                        pe.wait_ge(m_hb, 2 * a - 1 + n)
                    for d in range(KD):
                        last = pe.matmul(ps_h[:, n, :], xe_t[:, (k * KD + d) * P:(k * KD + d + 1) * P],
                                         w1_sb[:, ds(e * (KD * H) + d * H + n * 512, 512)],
                                         start=(d == 0), stop=(d == KD - 1))
                    last.then_inc(m_h, 1)

            def layer2(a, e):
                if not (isinstance(a, int) and a == 0):
                    pe.wait_ge(m_yb, a)
                pe.wait_ge(w2_in, e * 16 + 16)
                for j in range(KH):
                    if j % 4 == 0:
                        pe.wait_ge(m_htc, 2 * a + j // 4 + 1)
                    last = pe.matmul(ps_o[:, 0, 0:D], hid_t[:, j * P:(j + 1) * P],
                                     w2_sb[:, ds(e * (KH * D) + j * D, D)], start=(j == 0), stop=(j == KH - 1))
                last.then_inc(m_y, 1)

            def hidden_t(a):
                for n in range(2):
                    pe.wait_ge(m_gelu, 2 * a + n + 1)
                    if not (isinstance(a, int) and a == 0):
                        pe.wait_ge(m_htc, 2 * a - 1 + n)
                    for j in range(4):
                        last = pe.transpose(ps_ht[:, n, j * P:(j + 1) * P],
                                            hid[:, (4 * n + j) * P:(4 * n + j + 1) * P], ident[:, :])
                    last.then_inc(m_ht, 1)

            rows_t(0, 0, 16)

            def tile(a, k, rows_ahead):
                if rows_ahead is not None:
                    rows_t(a + 1, (k + 1) % 4, rows_ahead)
                layer1(a, k % 2, expert(a))
                if not (isinstance(a, int) and a == 0):
                    layer2(a - 1, expert(a - 1))
                hidden_t(a)

            for a in range(4):
                tile(a, a, 32 if a == 3 else 16)
            with pe.Fori(1, SURE // 4 - 1) as i:
                for k in range(4):
                    tile(4 * i + k, k, 16 * i + (32 if k == 3 else 16))
            for a in range(SURE - 4, SURE - 1):
                tile(a, a % 4, 16 * ((a + 1) // 4) + 16)
            def tiles_from(a):
                if a + 1 < MT:
                    with pe.If(used(a + 1)):
                        rows_t(a + 1, (a + 1) % 4, 16 * ((a + 1) // 4) + 16)
                tile(a, a % 4, None)
                if a + 1 < MT:
                    with pe.If(used(a + 1)):
                        tiles_from(a + 1)

            tiles_from(SURE - 1)
            last = pe.value_load(last_tile[0:1, 0:1], min_val=SURE, max_val=MT - 1)
            layer2(last, expert(last))


def kernel(x, src, dst, edge_weight, L0_gnn_w_nbr, L0_gnn_w_own, L0_gnn_bias, L0_ffn_Wr, L0_ffn_br, L0_ffn_ln_g,
           L0_ffn_ln_b, L0_ffn_W1, L0_ffn_b1, L0_ffn_W2, L0_ffn_b2):
    import numpy as np
    import concourse.bacc as bacc
    from concourse.bass_utils import run_bass_kernel_spmd

    n, d = x.shape
    rows = -(-n // P) * P
    per_it = 2 * CHUNKS_PER_GROUP * P
    edges = -(-len(src) // per_it) * per_it
    experts, _, hidden = L0_ffn_W1.shape

    def chunks(v, mode="constant"):
        return np.pad(np.asarray(v), (0, edges - len(v)), mode=mode).reshape(-1, P)

    dst_c = chunks(dst, "edge")
    arrays = {
        "x": np.pad(np.asarray(x), ((0, rows - n), (0, 0))),
        "src_t": np.ascontiguousarray(chunks(src).T),
        "dst_t": np.ascontiguousarray(dst_c.T),
        "dst_first": np.ascontiguousarray(dst_c[::CHUNKS_PER_GROUP, 0].reshape(1, -1)),
        "wgt_t": np.ascontiguousarray(chunks(edge_weight).T),
        "w_nbr": np.asarray(L0_gnn_w_nbr), "w_own": np.asarray(L0_gnn_w_own), "bias": np.asarray(L0_gnn_bias),
        "Wr": np.ascontiguousarray(np.asarray(L0_ffn_Wr).reshape(-1, P, experts).transpose(1, 0, 2).reshape(P, -1)),
        "br": np.asarray(L0_ffn_br),
        "ln_g": np.ascontiguousarray(np.asarray(L0_ffn_ln_g).reshape(experts, -1, P).transpose(2, 1, 0).reshape(P, -1)),
        "ln_b": np.ascontiguousarray(np.asarray(L0_ffn_ln_b).reshape(experts, -1, P).transpose(2, 1, 0).reshape(P, -1)),
        "W1": np.ascontiguousarray(np.asarray(L0_ffn_W1).reshape(experts, -1, P, hidden).transpose(2, 0, 1, 3)
                                   .reshape(P, -1)),
        "b1": np.asarray(L0_ffn_b1),
        "W2": np.ascontiguousarray(np.asarray(L0_ffn_W2).reshape(experts, -1, P, d).transpose(2, 0, 1, 3)
                                   .reshape(P, -1)),
        "b2": np.asarray(L0_ffn_b2),
    }
    nc = bacc.Bacc("TRN2", target_bir_lowering=False, num_devices=1)
    args = [nc.dram_tensor(k, v.shape, mybir.dt.from_np(v.dtype), kind="ExternalInput").ap()
            for k, v in arrays.items()]
    out = nc.dram_tensor("out", (rows + P, d), F32, kind="ExternalOutput").ap()
    gnn_moe(nc, *args, out)
    r = run_bass_kernel_spmd(nc, [arrays], core_ids=[0])
    return r.results[0]["out"][:n]
```
